# Optimizing a Trainium2 kernel written in Bass

```python
import numpy as np
import jax
import jax.numpy as jnp

def _softmax(x, axis=-1):
    return jax.nn.softmax(x, axis=axis)
def _gelu(x):
    return jax.nn.gelu(x, approximate=True)
def _silu(x):
    return jax.nn.silu(x)
def _sigmoid(x):
    return jax.nn.sigmoid(x)
def _layernorm(x, axis=-1, eps=1e-5):
    m = jnp.mean(x, axis=axis, keepdims=True)
    v = jnp.var(x, axis=axis, keepdims=True)
    return (x - m) / jnp.sqrt(v + eps)
def _scatter_add(tgt, idx, src, axis=0):
    return tgt.at[idx].add(src)
def _segment_sum(src, seg, n):
    return jax.ops.segment_sum(src, seg, n)

kernel_name = 'mk_adj_resnorm_d2_adj_512_573718'

def setup_inputs(seed: int = 0):
    np.random.seed(seed)
    _w = jnp.asarray
    def _rec_inputs():
        import jax
        import jax.numpy as jnp
        _gk = jax.random.key(seed)
        x = -0.000929 + 1 * jax.random.normal(jax.random.fold_in(_gk, 1), (64, 256, 512), jnp.float32)
        _a = jax.random.bernoulli(jax.random.fold_in(_gk, 2), 0.125, (256, 256))
        adj = _a.astype(jnp.int32)
        return x, adj
    x, adj = _rec_inputs()
    def _L0_gnn_setup():
        import jax, jax.numpy as jnp
        import numpy as np
        B, K, DIN, DOUT = (32, 64, 512, 512)
        key = jax.random.key(seed)
        k1, k2, k3, k4 = jax.random.split(key, 4)
        x = jax.random.normal(k1, (B, K, DIN), dtype=jnp.float32)
        adj = jax.random.randint(k2, (K, K), 0, 2, dtype=jnp.int32)
        W = jax.random.normal(k3, (DOUT, 2 * DIN), dtype=jnp.float32) * 0.02
        b = jax.random.normal(k4, (DOUT,), dtype=jnp.float32) * 0.02
        return {'x': x, 'adj': adj, 'W': W, 'b': b}
    _L0_gnn_all = _L0_gnn_setup()
    _L0_gnn_in = {k: v for k, v in _L0_gnn_all.items() if k in ('W', 'b', )}
    del _L0_gnn_all

    def _L1_gnn_setup():
        import jax, jax.numpy as jnp
        import numpy as np
        D_MODEL = 512
        NUM_HEADS = 8
        D_HEAD = D_MODEL // NUM_HEADS
        B, N = (4, 2048)
        key = jax.random.key(seed)
        ks = jax.random.split(key, 10)
        s = 1.0 / np.sqrt(D_MODEL)
        inp = {'h': jax.random.normal(ks[0], (B, N, D_MODEL), dtype=jnp.float32), 'adj': jax.random.randint(ks[1], (N, N), 0, 2, dtype=jnp.int32), 'Wq': jax.random.uniform(ks[2], (D_MODEL, D_MODEL), jnp.float32, -s, s), 'bq': jax.random.uniform(ks[3], (D_MODEL,), jnp.float32, -s, s), 'Wk': jax.random.uniform(ks[4], (D_MODEL, D_MODEL), jnp.float32, -s, s), 'bk': jax.random.uniform(ks[5], (D_MODEL,), jnp.float32, -s, s), 'Wv': jax.random.uniform(ks[6], (D_MODEL, D_MODEL), jnp.float32, -s, s), 'bv': jax.random.uniform(ks[7], (D_MODEL,), jnp.float32, -s, s), 'Wo': jax.random.uniform(ks[8], (D_MODEL, D_MODEL), jnp.float32, -s, s), 'bo': jax.random.uniform(ks[9], (D_MODEL,), jnp.float32, -s, s)}
        return inp
    _L1_gnn_all = _L1_gnn_setup()
    _L1_gnn_in = {k: v for k, v in _L1_gnn_all.items() if k in ('Wq', 'bq', 'Wk', 'bk', 'Wv', 'bv', 'Wo', 'bo', )}
    del _L1_gnn_all

    return {
        "x": x,
        "adj": adj,
        "L0_gnn_W": _L0_gnn_in["W"],
        "L0_gnn_b": _L0_gnn_in["b"],
        "L1_gnn_Wq": _L1_gnn_in["Wq"],
        "L1_gnn_bq": _L1_gnn_in["bq"],
        "L1_gnn_Wk": _L1_gnn_in["Wk"],
        "L1_gnn_bk": _L1_gnn_in["bk"],
        "L1_gnn_Wv": _L1_gnn_in["Wv"],
        "L1_gnn_bv": _L1_gnn_in["bv"],
        "L1_gnn_Wo": _L1_gnn_in["Wo"],
        "L1_gnn_bo": _L1_gnn_in["bo"],
    }

def reference(x, adj, L0_gnn_W, L0_gnn_b, L1_gnn_Wq, L1_gnn_bq, L1_gnn_Wk, L1_gnn_bk, L1_gnn_Wv, L1_gnn_bv, L1_gnn_Wo, L1_gnn_bo):
    import jax
    import jax.numpy as jnp
    def _L0_gnn_ref(x, adj, W, b):
        import jax, jax.numpy as jnp
        import numpy as np
        B, K, DIN, DOUT = (32, 64, 512, 512)
        Din = x.shape[-1]
        Wi, Wj = (W[:, :Din], W[:, Din:])
        mi = jnp.einsum('bkd,od->bko', x, Wi)
        mj = jnp.einsum('bkd,od->bko', x, Wj)
        a = adj.astype(x.dtype)
        deg = a.sum(axis=1)
        out = deg[None, :, None] * (mi + b) + jnp.einsum('ij,bjo->bio', a, mj)
        return out

    def _L1_gnn_ref(h, adj, Wq, bq, Wk, bk, Wv, bv, Wo, bo):
        import jax, jax.numpy as jnp
        import numpy as np
        D_MODEL = 512
        NUM_HEADS = 8
        D_HEAD = D_MODEL // NUM_HEADS
        B, N = (4, 2048)
        b, n, _ = h.shape

        def split_heads(x):
            return x.reshape(b, n, NUM_HEADS, D_HEAD).transpose(0, 2, 1, 3)
        q = split_heads(h @ Wq.T + bq)
        k = split_heads(h @ Wk.T + bk)
        v = split_heads(h @ Wv.T + bv)
        scale = 1.0 / np.sqrt(D_HEAD)
        scores = jnp.einsum('bhqd,bhkd->bhqk', q, k) * scale
        mask = (adj == 0)[None, None, :, :]
        scores = jnp.where(mask, -jnp.inf, scores)
        attn = jax.nn.softmax(scores, axis=-1)
        out = jnp.einsum('bhqk,bhkd->bhqd', attn, v)
        out = out.transpose(0, 2, 1, 3).reshape(b, n, D_MODEL)
        return out @ Wo.T + bo

    x = _layernorm(x + _L0_gnn_ref(x, adj, L0_gnn_W, L0_gnn_b), axis=-1)
    x = _layernorm(x + _L1_gnn_ref(x, adj, L1_gnn_Wq, L1_gnn_bq, L1_gnn_Wk, L1_gnn_bk, L1_gnn_Wv, L1_gnn_bv, L1_gnn_Wo, L1_gnn_bo), axis=-1)
    return x


_drawn_inputs = setup_inputs


def setup_inputs(seed=0):
    import zlib

    import numpy as np

    out = dict(_drawn_inputs(seed))
    spreads = {}
    factors = {'L1_gnn_Wq': 2.745,
     'L1_gnn_bq': 8.0,
     'L1_gnn_Wk': 2.742,
     'L1_gnn_bk': 8.0,
     'L1_gnn_bv': 3.887}
    for name, (base, spread) in spreads.items():
        noise = np.random.default_rng([zlib.crc32(name.encode()), seed]).standard_normal(out[name].shape)
        drawn = base * np.exp(spread * noise) if base else spread * noise
        out[name] = jnp.asarray(drawn.astype(out[name].dtype))
    for name, factor in factors.items():
        out[name] = (out[name] * factor).astype(out[name].dtype)
    return out
```

```python
from contextlib import ExitStack

import concourse.bass as bass
from concourse import mybir

F32 = mybir.dt.float32
F32R = mybir.dt.float32r
I32 = mybir.dt.int32
ALU = mybir.AluOpType
ACT = mybir.ActivationFunctionType
AX_X = mybir.AxisListType.X

P = 128
HEADS = 8
EPS = 1e-5
MASKED = -3.0e38
MAX_FLOOR = -1.0e37
WEIGHTS = ("wj", "wi", "wq", "wk", "wv", "wo")


def build(nc, x, xT, adj, adjT, w0T, b0, wqT, wkT, wvT, woT, bq, bk, bv, bo, out):
    B, N, D = x.shape
    DH = D // HEADS
    R = N // P
    C = D // P
    G = HEADS // 2
    HALF = P // 2
    SCALE = float(DH) ** -0.5
    assert (R, C, G, DH) == (2, 4, 4, HALF) and B % 2 == 0 and B >= 6

    x_rows = x.rearrange("b (r p) d -> b p r d", p=P)
    xT_cols = xT.rearrange("b (c p) n -> b p c n", p=P)
    out_rows = out.rearrange("b (r p) d -> b p r d", p=P)
    w_dram = {
        "wi": w0T[0:D, :], "wj": w0T[D:2 * D, :], "wq": wqT, "wk": wkT, "wv": wvT, "wo": woT,
    }

    with ExitStack() as ctx:
        def sb(name, shape, dt=F32):
            return ctx.enter_context(nc.sbuf_tensor(name, shape, dt))

        def sem(name):
            return ctx.enter_context(nc.semaphore(name))

        def bank(name):
            return ctx.enter_context(nc.psum_tensor(name, [P, 512], F32))

        w_hi = {k: sb(f"{k}_hi", [P, C, D], F32R) for k in WEIGHTS}
        w_lo = {k: sb(f"{k}_lo", [P, C, D], F32R) for k in WEIGHTS}
        aT = sb("aT", [P, R, N], F32R)
        mask_add = sb("mask_add", [P, R, N])
        deg = sb("deg", [P, R])
        deg_b0 = sb("deg_b0", [P, R, D])
        bo_rows = sb("bo_rows", [P, D])
        ident = sb("ident", [P, P])
        eps_cols = sb("eps_cols", [P, R])
        power_cols = sb("power_cols", [P, R])
        bq_cols = sb("bq_cols", [P, C])
        bk_cols = sb("bk_cols", [P, C])
        bv_cols = sb("bv_cols", [HALF, HEADS])

        xT_raw = sb("xT_raw", [P, C, N])
        xT_hi = sb("xT_hi", [P, C, N], F32R)
        xT_lo = sb("xT_lo", [P, C, N], F32R)
        xb = sb("xb", [P, R, D])
        mj_hi = sb("mj_hi", [P, R, D], F32R)
        mj_lo = sb("mj_lo", [P, R, D], F32R)
        h = sb("h", [P, R, D])
        hb = sb("hb", [P, 2, R, D])
        hT_hi = sb("hT_hi", [P, C, N], F32R)
        hT_lo = sb("hT_lo", [P, C, N], F32R)
        q_both = sb("q_both", [P, HEADS, N], F32R)
        k_twice = sb("k_twice", [P, HEADS, N], F32R)
        k_lo = sb("k_lo", [P, C, N], F32R)
        v_both = sb("v_both", [P, R, HEADS, 2 * DH], F32R)
        probs = sb("probs", [P, 2, 2, R, N])
        pT_hi = sb("pT_hi", [P, 2, R, N], F32R)
        pT_lo = sb("pT_lo", [P, 2, R, N], F32R)
        o_part = sb("o_part", [HALF, 2, N])
        oT = sb("oT", [P, N])
        oT_hi = sb("oT_hi", [P, G, N], F32R)
        oT_lo = sb("oT_lo", [P, G, N], F32R)
        row_max = sb("row_max", [P, 2, 2 * R])
        exp_bias = sb("exp_bias", [P, 2, 2 * R])
        row_sum = sb("row_sum", [P, 2, 2 * R])
        row_inv = sb("row_inv", [P, 2, 2 * R])
        stats = {k: sb(f"stats_{k}", [P, R, 6]) for k in ("h", "out")}
        mean_var = {k: sb(f"mean_var_{k}", [P, R, 2]) for k in ("h", "out")}
        var_eps = {k: sb(f"var_eps_{k}", [P, R]) for k in ("h", "out")}
        rstd = {k: sb(f"rstd_{k}", [P, R]) for k in ("h", "out")}

        stage = [probs[:, :, :, :, :].rearrange("p a b c d -> p (a b c d)"),
                 hb[:, :, :, :].rearrange("p a b c -> p (a b c)")]
        adj_i = xb[:, 0, :].bitcast(I32)
        adjT_i = xb[:, 1, :].bitcast(I32)
        adj_f = h[:, 0, :]
        b0_rows = h[:, 1, :]

        proj = [bank(f"proj{i}") for i in range(3)]
        score = [bank(f"score{i}") for i in range(2)]
        pt = [bank(f"pt{i}") for i in range(2)]
        av = bank("av")
        BANK = {"mj": (0, 1), "mi": (2, 0), "agg": (1, 2), "y": (0, 1), "hT": (2, 0),
                "q": (1, 2), "k": (0, 1), "v": (2, 1)}

        w_loaded = [sem("w_loaded0"), sem("w_loaded1")]
        w_hi_done, w_split = sem("w_hi_done"), sem("w_split")
        const_loaded, bias_loaded = sem("const_loaded"), sem("bias_loaded")
        zeroed, ident_ready = sem("zeroed"), sem("ident_ready")
        adj_ready, deg_ready, deg_b0_ready = sem("adj_ready"), sem("deg_ready"), sem("deg_b0_ready")
        xT_loaded, x_loaded, out_stored = sem("xT_loaded"), sem("x_loaded"), sem("out_stored")
        xT_hi_done, xT_split = sem("xT_hi_done"), sem("xT_split")
        xb_ready, hb_ready, o_split = sem("xb_ready"), sem("hb_ready"), sem("o_split")
        done = {k: sem(f"{k}_done") for k in BANK}
        score_done, pt_done, av_done = sem("score_done"), sem("pt_done"), sem("av_done")
        hi = {k: sem(f"{k}_hi_done") for k in ("mj", "hT", "q", "k", "v")}
        exp_done, norm_done, pt_hi_done = sem("exp_done"), sem("norm_done"), sem("pt_hi_done")
        o_part_done, o_hi_done = sem("o_part_done"), sem("o_hi_done")
        read = {k: sem(f"{k}_read") for k in BANK}
        max_done, bias_done, inv_done = sem("max_done"), sem("bias_done"), sem("inv_done")
        pt_read, av_read = sem("pt_read"), sem("av_read")
        stats_done = {k: sem(f"stats_{k}_done") for k in ("h", "out")}
        aggr_done = {k: sem(f"aggr_{k}_done") for k in ("h", "out")}
        var_eps_done = {k: sem(f"var_eps_{k}_done") for k in ("h", "out")}
        rstd_done = {k: sem(f"rstd_{k}_done") for k in ("h", "out")}
        normed = {k: sem(f"normed_{k}") for k in ("h", "out")}

        def steps(eng, step):
            step(0, parity=0, y_=False)
            with eng.Fori(0, (B - 4) // 2) as i:
                step(2 * i + 1, parity=1)
                step(2 * i + 2, parity=0)
            step(B - 3, parity=1)
            step(B - 2, parity=0, ahead=False)
            step(B - 1, parity=1, ahead=False, proj=False)

        block = ctx.enter_context(nc.Block())

        @block.sync
        def _(sp):
            def load_xT(n):
                sp.dma_start(xT_raw[:, :, :], xT_cols[n, :, :, :]).then_inc(xT_loaded, 16)

            def load_x(n):
                sp.dma_start(xb[:, :, :], x_rows[n, :, :, :]).then_inc(x_loaded, 16)

            def store(b, parity):
                sp.wait_ge(normed["out"], R * (b + 1))
                sp.dma_start(out_rows[b, :, :, :], hb[:, parity, :, :]).then_inc(out_stored, 16)

            def step(b, parity, y_=True, ahead=True, proj=True):
                if ahead:
                    sp.wait_ge(xT_split, b + 2)
                    load_xT(b + 2)
                if proj:
                    sp.wait_ge(read["mi"], R * (b + 1))
                    load_x(b + 1)
                if y_:
                    store(b - 1, 1 - parity)

            sp.dma_start(adj_i.rearrange("p (r n) -> p r n", r=R),
                         adj.rearrange("(r p) n -> p r n", p=P)).then_inc(const_loaded, 16)
            sp.dma_start(adjT_i.rearrange("p (r n) -> p r n", r=R),
                         adjT.rearrange("(r p) n -> p r n", p=P)).then_inc(const_loaded, 16)
            sp.dma_start(b0_rows, b0.partition_broadcast(P)).then_inc(const_loaded, 16)
            load_xT(0)
            for i, k in enumerate(WEIGHTS):
                if i >= 2:
                    sp.wait_ge(w_split, i - 1)
                sp.dma_start(stage[i % 2].rearrange("p (c o) -> p c o", c=C),
                             w_dram[k].rearrange("(c p) o -> p c o", p=P)).then_inc(w_loaded[i % 2], 16)
                if i == 1:
                    sp.dma_start(bo_rows[:, :], bo.partition_broadcast(P)).then_inc(bias_loaded, 16)
                    sp.dma_start(bq_cols[:, :], bq).then_inc(bias_loaded, 16)
                    sp.dma_start(bk_cols[:, :], bk).then_inc(bias_loaded, 16)
                    sp.dma_start(bv_cols[:, :], bv).then_inc(bias_loaded, 16)
                    sp.wait_ge(adj_ready, 3)
                    load_x(0)
                    sp.wait_ge(xT_split, 1)
                    load_xT(1)
            steps(sp, step)
            store(B - 1, (B - 1) % 2)
            sp.wait_ge(out_stored, 16 * B)

        @block.gpsimd
        def _(pool):
            def split_xT(n):
                pool.wait_ge(xT_hi_done, n + 1)
                pool.tensor_tensor(xT_lo[:, :, :], xT_raw[:, :, :], xT_hi[:, :, :].bitcast(F32),
                                   ALU.subtract).then_inc(xT_split, 1)

            def add_bias(n):
                pool.wait_ge(x_loaded, 16 * (n + 1))
                pool.tensor_tensor(xb[:, :, :], xb[:, :, :], deg_b0[:, :, :], ALU.add).then_inc(xb_ready, 1)

            def residual(n, parity, stored):
                pool.wait_ge(normed["h"], R * (n + 1))
                if stored:
                    pool.wait_ge(out_stored, 16 * (n - 1))
                for r in range(R):
                    last = pool.tensor_tensor(hb[:, parity, r, :], h[:, r, :], bo_rows[:, :], ALU.add)
                last.then_inc(hb_ready, 1)

            def root(which, n):
                pool.wait_ge(aggr_done[which], R * n + R)
                pool.tensor_tensor(var_eps[which][:, :], mean_var[which][:, :, 1], eps_cols[:, :],
                                   ALU.add).then_inc(var_eps_done[which], 1)
                pool.wait_ge(var_eps_done[which], n + 1)
                pool.tensor_tensor(rstd[which][:, :], var_eps[which][:, :], power_cols[:, :],
                                   ALU.pow).then_inc(rstd_done[which], 1)

            def split_o(b, g):
                pool.wait_ge(o_hi_done, G * b + g + 1)
                pool.tensor_tensor(oT_lo[:, g, :], oT[:, :], oT_hi[:, g, :].bitcast(F32),
                                   ALU.subtract).then_inc(o_split, 1)

            pool.memset(ident[:, :], 0.0).then_inc(zeroed, 1)
            pool.wait_ge(zeroed, 1)
            pool.affine_select(out=ident[:, :], in_=ident[:, :], compare_op=ALU.not_equal, fill=1.0, base=0,
                               pattern=[[-1, P]], channel_multiplier=1).then_inc(ident_ready, 1)
            pool.memset(eps_cols[:, :], EPS).then_inc(zeroed, 1)
            pool.memset(power_cols[:, :], -0.5).then_inc(zeroed, 1)
            split_xT(0)
            pool.wait_ge(zeroed, 3)
            pool.wait_ge(deg_b0_ready, R)
            add_bias(0)
            root("h", 0)
            split_xT(1)
            pool.wait_ge(bias_loaded, 64)
            pool.wait_ge(w_split, len(WEIGHTS))
            residual(0, 0, stored=False)

            def step(b, parity, y_=True, ahead=True, proj=True):
                n = b + 1
                if proj: add_bias(n)
                if proj: root("h", n)
                if y_: root("out", b - 1)
                split_o(b, 0)
                if ahead: split_xT(b + 2)
                split_o(b, 1)
                split_o(b, 2)
                if proj: residual(n, 1 - parity, stored=y_)
                split_o(b, 3)

            steps(pool, step)
            root("out", B - 1)

        @block.tensor
        def _(pe):
            def mm(dst, lhsT, rhs, start, stop):
                return pe.matmul(dst, lhsT, rhs, start=start, stop=stop)

            def product(dst, l_hi, l_lo, r_hi, r_lo):
                terms = [(a(c), b(c)) for c in range(C) for a, b in ((l_hi, r_hi), (l_lo, r_hi), (l_hi, r_lo))]
                for i, (a, b) in enumerate(terms):
                    last = mm(dst, a, b, i == 0, i == len(terms) - 1)
                return last

            def rows_times_w(kind, r, l_hi, l_lo, w):
                rows = slice(r * P, (r + 1) * P)
                product(proj[BANK[kind][r]][:, :], lambda c: l_hi[:, c, rows], lambda c: l_lo[:, c, rows],
                        lambda c: w_hi[w][:, c, :], lambda c: w_lo[w][:, c, :]).then_inc(done[kind], 1)

            def mj(n, first=False):
                pe.wait_ge(xT_split, n + 1)
                if first:
                    pe.wait_ge(w_split, 1)
                else:
                    pe.wait_ge(read["k"], 2 * n - 1)
                rows_times_w("mj", 0, xT_hi, xT_lo, "wj")
                if not first:
                    pe.wait_ge(read["v"], R * n)
                rows_times_w("mj", 1, xT_hi, xT_lo, "wj")

            def mi(n, first=False):
                if first:
                    pe.wait_ge(w_split, 2)
                rows_times_w("mi", 0, xT_hi, xT_lo, "wi")
                pe.wait_ge(read["mj"], R * n + 1)
                rows_times_w("mi", 1, xT_hi, xT_lo, "wi")

            def aggregate(n, first=False):
                pe.wait_ge(read["mj"], R * n + 2)
                for r in range(R):
                    if r == 1:
                        pe.wait_ge(read["mi"], R * n + 1)
                    dst = proj[BANK["agg"][r]][:, :]
                    terms = [(aT[:, j, r * P:(r + 1) * P], half[:, j, :]) for j in range(R) for half in (mj_hi, mj_lo)]
                    for i, (a, m) in enumerate(terms):
                        last = mm(dst, a, m, i == 0, i == len(terms) - 1)
                    last.then_inc(done["agg"], 1)

            def y(b):
                pe.wait_ge(o_split, G * (b + 1))
                pe.wait_ge(read["mi"], R * (b + 3) if type(b) is not int or b < B - 2 else R * B)
                rows_times_w("y", 0, oT_hi, oT_lo, "wo")
                pe.wait_ge(read["agg"], R * (b + 2) + 1 if type(b) is not int or b < B - 2 else R * B)
                rows_times_w("y", 1, oT_hi, oT_lo, "wo")

            def transpose_h(n, first=False):
                pe.wait_ge(normed["h"], R * (n + 1))
                if first:
                    pe.wait_ge(ident_ready, 1)
                for half in range(2):
                    if half == 1 and not first:
                        y_before(n)
                    dst = proj[BANK["hT"][half]][:, :].rearrange("p (c n) -> p c n", c=2)
                    for c in range(2):
                        for r in range(R):
                            last = pe.transpose(dst[:, c, r * P:(r + 1) * P],
                                                h[:, r, (2 * half + c) * P:(2 * half + c + 1) * P], ident[:, :])
                    last.then_inc(done["hT"], 1)

            def y_before(n):
                if type(n) is not int or n >= 2:
                    pe.wait_ge(read["y"], R * (n - 2) + 1)

            def cols_of(kind, n, half, w):
                dst = proj[BANK[kind][half]][:, :].rearrange("p (c n) -> p c n", c=2)
                for c in range(2):
                    cols = slice((2 * half + c) * P, (2 * half + c + 1) * P)
                    last = product(dst[:, c, :], lambda k: w_hi[w][:, k, cols], lambda k: w_lo[w][:, k, cols],
                                   lambda k: hT_hi[:, k, :], lambda k: hT_lo[:, k, :])
                last.then_inc(done[kind], 1)

            def q(n, first=False):
                if first:
                    pe.wait_ge(w_split, 3)
                pe.wait_ge(read["hT"], 2 * n + 2)
                if type(n) is not int or n >= 2:
                    pe.wait_ge(read["y"], R * (n - 1))
                cols_of("q", n, 0, "wq")
                cols_of("q", n, 1, "wq")

            def k(n, half, first=False):
                if first:
                    pe.wait_ge(w_split, 4)
                if half == 1:
                    pe.wait_ge(read["q"], 2 * n + 1)
                cols_of("k", n, half, "wk")

            def v(n, first=False):
                if first:
                    pe.wait_ge(w_split, 5)
                pe.wait_ge(read["q"], 2 * n + 2)
                rows_times_w("v", 0, hT_hi, hT_lo, "wv")
                pe.wait_ge(read["k"], 2 * n + 2)
                rows_times_w("v", 1, hT_hi, hT_lo, "wv")

            def scores(b, g, first=False):
                pe.wait_ge(read["q"], 2 * b + g // 2 + 1)
                pe.wait_ge(read["k"], 2 * b + g // 2 + 1)
                if not (first and g == 0):
                    pe.wait_ge(max_done, 2 * (G * b + g))
                blocks = [(i, r) for i in range(2) for r in range(R)]
                for i, r in blocks:
                    head = 2 * g + i
                    pe.matmul(score[i][:, r * N:(r + 1) * N], q_both[:, head, r * P:(r + 1) * P],
                              k_twice[:, head, :], start=(r == 0), stop=False, skip_group_check=True)
                for i, r in blocks:
                    head, home = 2 * g + i, slice(i * HALF, (i + 1) * HALF)
                    last = pe.matmul(score[i][:, r * N:(r + 1) * N], q_both[home, head, r * P:(r + 1) * P],
                                     k_lo[home, g, :], start=False, stop=True, skip_group_check=True)
                    if r == R - 1:
                        last.then_inc(score_done, 1)

            def transpose_p(b, g, first=False):
                for i in range(2):
                    pe.wait_ge(norm_done, 2 * (G * b + g) + i + 1)
                    if not (first and g == 0):
                        pe.wait_ge(pt_read, 2 * (G * b + g) + i - 1)
                    dst = pt[i][:, :].rearrange("p (k q) -> p k q", k=R)
                    for kt in range(R):
                        for r in range(R):
                            last = pe.transpose(dst[:, kt, r * P:(r + 1) * P],
                                                probs[:, g % 2, i, r, kt * P:(kt + 1) * P], ident[:, :])
                    last.then_inc(pt_done, 1)

            def attend(b, g, first=False):
                if g == 0:
                    pe.wait_ge(read["v"], R * (b + 1))
                pe.wait_ge(pt_read, 2 * (G * b + g) + 2)
                if not (first and g == 0):
                    pe.wait_ge(av_read, G * b + g)
                for i in range(2):
                    terms = [(kt, half) for kt in range(R) for half in (pT_hi, pT_lo)]
                    for j, (kt, half) in enumerate(terms):
                        last = mm(av[:, i * N:(i + 1) * N], v_both[:, kt, 2 * g + i, :], half[:, i, kt, :],
                                  j == 0, j == len(terms) - 1)
                last.then_inc(av_done, 1)

            def step(b, parity, y_=True, ahead=True, proj=True):
                n = b + 1
                scores(b, 0, not y_)
                if proj: mj(n)
                scores(b, 1)
                if proj: mi(n)
                transpose_p(b, 0, not y_)
                scores(b, 2)
                if proj: aggregate(n)
                if y_: y(b - 1)
                if proj: transpose_h(n)
                attend(b, 0, not y_)
                transpose_p(b, 1)
                scores(b, 3)
                if proj: q(n)
                attend(b, 1)
                transpose_p(b, 2)
                if proj: k(n, 0)
                attend(b, 2)
                transpose_p(b, 3)
                if proj: k(n, 1)
                attend(b, 3)
                if proj: v(n)

            mj(0, first=True)
            mi(0, first=True)
            aggregate(0)
            transpose_h(0, first=True)
            q(0, first=True)
            k(0, 0, first=True)
            k(0, 1)
            v(0, first=True)
            pe.wait_ge(w_split, len(WEIGHTS))
            steps(pe, step)
            y(B - 1)

        @block.scalar
        def _(act):
            def copy_hi(kind, n, tile, dst, src):
                act.wait_ge(done[kind], 2 * n + tile + 1)
                nc.scalar.copy(dst, src).then_inc(hi[kind], 1)

            def mj_high(n, r):
                copy_hi("mj", n, r, mj_hi[:, r, :], proj[BANK["mj"][r]][:, :])

            def hT_high(n, half):
                copy_hi("hT", n, half, hT_hi[:, 2 * half:2 * half + 2, :],
                        proj[BANK["hT"][half]][:, :].rearrange("p (c n) -> p c n", c=2))

            def v_high(n, r):
                copy_hi("v", n, r, v_both[:, r, :, 0:DH],
                        proj[BANK["v"][r]][:, :].rearrange("p (h d) -> p h d", h=HEADS))

            def q_high(n, half):
                act.wait_ge(done["q"], 2 * n + half + 1)
                for c in range(2):
                    t = 2 * half + c
                    src = proj[BANK["q"][half]][:, c * N:(c + 1) * N]
                    for i in range(2):
                        home = slice(i * HALF, (i + 1) * HALF)
                        last = nc.scalar.activation(q_both[home, 2 * t + i, :], src[home, :], ACT.Identity,
                                                    bias=bq_cols[home, t:t + 1])
                last.then_inc(hi["q"], 1)

            def k_high(n, half):
                act.wait_ge(done["k"], 2 * n + half + 1)
                for c in range(2):
                    t = 2 * half + c
                    src = proj[BANK["k"][half]][:, c * N:(c + 1) * N]
                    for i in range(2):
                        home = slice(i * HALF, (i + 1) * HALF)
                        away = slice((1 - i) * HALF, (2 - i) * HALF)
                        for to in (home, away):
                            last = nc.scalar.activation(k_twice[to, 2 * t + i, :], src[home, :], ACT.Identity,
                                                        bias=bk_cols[home, t:t + 1])
                last.then_inc(hi["k"], 1)

            def exponentials(b, g):
                act.wait_ge(bias_done, G * b + g + 1)
                for i in range(2):
                    for r in range(R):
                        s = R * i + r
                        e = probs[:, g % 2, i, r, :]
                        last = nc.scalar.activation(e, e, ACT.Exp, bias=exp_bias[:, g % 2, s:s + 1], scale=SCALE,
                                                    accum_out=row_sum[:, g % 2, s:s + 1])
                last.then_inc(exp_done, 1)

            def normalise(b, g):
                act.wait_ge(inv_done, G * b + g + 1)
                for i in range(2):
                    for r in range(R):
                        s = R * i + r
                        e = probs[:, g % 2, i, r, :]
                        last = nc.scalar.activation(e, e, ACT.Copy, scale=row_inv[:, g % 2, s:s + 1])
                    last.then_inc(norm_done, 1)

            def pt_high(b, g, first=False):
                for i in range(2):
                    act.wait_ge(pt_done, 2 * (G * b + g) + i + 1)
                    if i == 0 and not (first and g == 0):
                        act.wait_ge(av_done, G * b + g)
                    nc.scalar.copy(pT_hi[:, i, :, :],
                                   pt[i][:, :].rearrange("p (k q) -> p k q", k=R)).then_inc(pt_hi_done, 1)

            def o_low_part(b, g, first=False):
                act.wait_ge(av_done, G * b + g + 1)
                if not (first and g == 0):
                    act.wait_ge(av_read, G * b + g)
                nc.scalar.copy(o_part[:, :, :],
                               av[HALF:P, :].rearrange("p (i n) -> p i n", i=2)).then_inc(o_part_done, 1)

            def o_high(b, g, first=False):
                act.wait_ge(av_read, G * b + g + 1)
                if g == 0 and not first:
                    act.wait_ge(done["y"], R * b)
                nc.scalar.copy(oT_hi[:, g, :], oT[:, :]).then_inc(o_hi_done, 1)

            def xT_high(n):
                act.wait_ge(xT_loaded, 16 * (n + 1))
                if type(n) is not int or n > 0:
                    act.wait_ge(done["mi"], R * n)
                nc.scalar.copy(xT_hi[:, :, :], xT_raw[:, :, :]).then_inc(xT_hi_done, 1)

            def step(b, parity, y_=True, ahead=True, proj=True):
                n = b + 1
                exponentials(b, 0)
                if proj: mj_high(n, 0)
                normalise(b, 0)
                if proj: mj_high(n, 1)
                exponentials(b, 1)
                normalise(b, 1)
                pt_high(b, 0, not y_)
                exponentials(b, 2)
                if ahead: xT_high(b + 2)
                normalise(b, 2)
                if proj: hT_high(n, 0)
                if proj: hT_high(n, 1)
                o_low_part(b, 0, not y_)
                pt_high(b, 1)
                o_high(b, 0, not y_)
                if proj: q_high(n, 0)
                exponentials(b, 3)
                if proj: q_high(n, 1)
                normalise(b, 3)
                o_low_part(b, 1)
                pt_high(b, 2)
                o_high(b, 1)
                if proj: k_high(n, 0)
                o_low_part(b, 2)
                pt_high(b, 3)
                o_high(b, 2)
                if proj: k_high(n, 1)
                o_low_part(b, 3)
                o_high(b, 3)
                if proj: v_high(n, 0)
                if proj: v_high(n, 1)

            def split_weight(i):
                act.wait_ge(w_loaded[i % 2], 16 * (i // 2 + 1))
                nc.scalar.copy(w_hi[WEIGHTS[i]][:, :, :],
                               stage[i % 2].rearrange("p (c o) -> p c o", c=C)).then_inc(w_hi_done, 1)

            xT_high(0)
            split_weight(0)
            split_weight(1)
            mj_high(0, 0)
            mj_high(0, 1)
            for i in range(2, len(WEIGHTS)):
                split_weight(i)
            xT_high(1)
            hT_high(0, 0)
            hT_high(0, 1)
            act.wait_ge(bias_loaded, 64)
            q_high(0, 0)
            q_high(0, 1)
            k_high(0, 0)
            k_high(0, 1)
            v_high(0, 0)
            v_high(0, 1)
            steps(act, step)

        @block.vector
        def _(dve):
            V = nc.vector

            def low(kind, n, tile, dst, src, high):
                dve.wait_ge(hi[kind], 2 * n + tile + 1)
                V.tensor_tensor(dst, src, high.bitcast(F32), ALU.subtract).then_inc(read[kind], 1)

            def mj_low(n, r):
                low("mj", n, r, mj_lo[:, r, :], proj[BANK["mj"][r]][:, :], mj_hi[:, r, :])

            def hT_low(n, half):
                cs = slice(2 * half, 2 * half + 2)
                low("hT", n, half, hT_lo[:, cs, :],
                    proj[BANK["hT"][half]][:, :].rearrange("p (c n) -> p c n", c=2), hT_hi[:, cs, :])

            def v_low(n, r):
                low("v", n, r, v_both[:, r, :, DH:2 * DH],
                    proj[BANK["v"][r]][:, :].rearrange("p (h d) -> p h d", h=HEADS), v_both[:, r, :, 0:DH])

            def biased_low(kind, n, half, bias, high, dst):
                dve.wait_ge(hi[kind], 2 * n + half + 1)
                for c in range(2):
                    t = 2 * half + c
                    src = proj[BANK[kind][half]][:, c * N:(c + 1) * N]
                    for i in range(2):
                        home = slice(i * HALF, (i + 1) * HALF)
                        last = V.scalar_tensor_tensor(
                            out=dst(t, i), in0=src[home, :], scalar=bias[home, t:t + 1],
                            in1=high[home, 2 * t + i, :].bitcast(F32), op0=ALU.add, op1=ALU.subtract)
                last.then_inc(read[kind], 1)

            def q_low(n, half):
                biased_low("q", n, half, bq_cols, q_both,
                           lambda t, i: q_both[(1 - i) * HALF:(2 - i) * HALF, 2 * t + i, :])

            def k_low_half(n, half):
                biased_low("k", n, half, bk_cols, k_twice,
                           lambda t, i: k_lo[i * HALF:(i + 1) * HALF, t, :])

            def maxima(b, g, first=False):
                for i in range(2):
                    dve.wait_ge(score_done, 2 * (G * b + g) + i + 1)
                    if i == 0 and not (first and g < 2):
                        dve.wait_ge(pt_done, 2 * (G * b + g) - 2)
                    dve.nop(nofuse=True)
                    for r in range(R):
                        s = R * i + r
                        last = V.tensor_tensor_reduce(
                            out=probs[:, g % 2, i, r, :], in0=score[i][:, r * N:(r + 1) * N],
                            in1=mask_add[:, r, :], scale=1.0, scalar=MASKED, op0=ALU.add, op1=ALU.max,
                            accum_out=row_max[:, g % 2, s:s + 1])
                    last.then_inc(max_done, 1)
                dve.wait_ge(max_done, 2 * (G * b + g) + 2)
                V.tensor_scalar(exp_bias[:, g % 2, :], row_max[:, g % 2, :], MAX_FLOOR, -SCALE,
                                ALU.max, ALU.mult).then_inc(bias_done, 1)

            def inverse_sums(b, g):
                dve.wait_ge(exp_done, G * b + g + 1)
                V.reciprocal(row_inv[:, g % 2, :], row_sum[:, g % 2, :]).then_inc(inv_done, 1)

            def pt_low(b, g):
                for i in range(2):
                    dve.wait_ge(pt_hi_done, 2 * (G * b + g) + i + 1)
                    V.tensor_tensor(pT_lo[:, i, :, :], pt[i][:, :].rearrange("p (k q) -> p k q", k=R),
                                    pT_hi[:, i, :, :].bitcast(F32), ALU.subtract).then_inc(pt_read, 1)

            def o_sum(b, g, first=False):
                dve.wait_ge(o_part_done, G * b + g + 1)
                if not (first and g == 0):
                    dve.wait_ge(o_split, G * b + g)
                for i in range(2):
                    last = V.scalar_tensor_tensor(
                        out=oT[i * HALF:(i + 1) * HALF, :], in0=av[0:HALF, i * N:(i + 1) * N],
                        scalar=bv_cols[:, 2 * g + i:2 * g + i + 1], in1=o_part[:, i, :],
                        op0=ALU.add, op1=ALU.add)
                last.then_inc(av_read, 1)

            def mi_sum(n, r, first=False):
                dve.wait_ge(done["mi"], R * n + r + 1)
                dve.wait_ge(xb_ready, n + 1)
                if not first:
                    dve.wait_ge(hb_ready, n)
                V.scalar_tensor_tensor(out=h[:, r, :], in0=proj[BANK["mi"][r]][:, :], scalar=deg[:, r:r + 1],
                                       in1=xb[:, r, :], op0=ALU.mult, op1=ALU.add).then_inc(read["mi"], 1)

            def agg_sum(n, r):
                dve.wait_ge(done["agg"], R * n + r + 1)
                dve.wait_ge(read["mi"], R * n + r + 1)
                V.tensor_tensor(h[:, r, :], proj[BANK["agg"][r]][:, :], h[:, r, :],
                                ALU.add).then_inc(read["agg"], 1)

            def y_sum(b, r, parity):
                dve.wait_ge(done["y"], R * b + r + 1)
                dve.wait_ge(hb_ready, b + 1)
                V.tensor_tensor(hb[:, parity, r, :], proj[BANK["y"][r]][:, :], hb[:, parity, r, :],
                                ALU.add).then_inc(read["y"], 1)

            h_row = lambda r: h[:, r, :]
            hb_row = [lambda r: hb[:, 0, r, :], lambda r: hb[:, 1, r, :]]

            def norm_stats(which, n, r, summed, row):
                dve.wait_ge(summed, R * n + r + 1)
                V.bn_stats(stats[which][:, r, :], row(r)).then_inc(stats_done[which], 1)

            def norm_mean(which, n):
                dve.wait_ge(stats_done[which], R * n + R)
                dve.nop(nofuse=True)
                for r in range(R):
                    V.bn_aggr(mean_var[which][:, r, :], stats[which][:, r, :]).then_inc(aggr_done[which], 1)

            def norm_apply(which, n, row):
                dve.wait_ge(rstd_done[which], n + 1)
                for r in range(R):
                    V.tensor_scalar(row(r), row(r), mean_var[which][:, r, 0:1], rstd[which][:, r:r + 1],
                                    ALU.subtract, ALU.mult).then_inc(normed[which], 1)

            def step(b, parity, y_=True, ahead=True, proj=True):
                n, other = b + 1, 1 - parity
                maxima(b, 0, not y_)
                if proj: mj_low(n, 0)
                inverse_sums(b, 0)
                if proj: mj_low(n, 1)
                maxima(b, 1, not y_)
                if proj: mi_sum(n, 0)
                inverse_sums(b, 1)
                if proj: mi_sum(n, 1)
                pt_low(b, 0)
                maxima(b, 2)
                if proj: agg_sum(n, 0)
                if proj: agg_sum(n, 1)
                if proj: norm_stats("h", n, 0, read["agg"], h_row)
                if proj: norm_stats("h", n, 1, read["agg"], h_row)
                if proj: norm_mean("h", n)
                inverse_sums(b, 2)
                if proj: norm_apply("h", n, h_row)
                if y_: y_sum(b - 1, 0, other)
                if y_: y_sum(b - 1, 1, other)
                if y_: norm_stats("out", b - 1, 0, read["y"], hb_row[other])
                if proj: hT_low(n, 0)
                if proj: hT_low(n, 1)
                o_sum(b, 0, not y_)
                pt_low(b, 1)
                maxima(b, 3)
                if y_: norm_stats("out", b - 1, 1, read["y"], hb_row[other])
                if y_: norm_mean("out", b - 1)
                if proj: q_low(n, 0)
                inverse_sums(b, 3)
                if proj: q_low(n, 1)
                if y_: norm_apply("out", b - 1, hb_row[other])
                o_sum(b, 1)
                pt_low(b, 2)
                if proj: k_low_half(n, 0)
                o_sum(b, 2)
                pt_low(b, 3)
                if proj: k_low_half(n, 1)
                o_sum(b, 3)
                if proj: v_low(n, 0)
                if proj: v_low(n, 1)

            def split_weight(i):
                dve.wait_ge(w_hi_done, i + 1)
                V.tensor_tensor(w_lo[WEIGHTS[i]][:, :, :], stage[i % 2].rearrange("p (c o) -> p c o", c=C),
                                w_hi[WEIGHTS[i]][:, :, :].bitcast(F32), ALU.subtract).then_inc(w_split, 1)

            dve.wait_ge(const_loaded, 48)
            V.tensor_copy(aT[:, :, :], adjT_i.rearrange("p (r n) -> p r n", r=R)).then_inc(adj_ready, 1)
            V.tensor_copy(adj_f, adj_i).then_inc(adj_ready, 1)
            dve.wait_ge(adj_ready, 2)
            V.tensor_scalar(mask_add[:, :, :], adj_f.rearrange("p (r n) -> p r n", r=R), 0.0, MASKED,
                            ALU.is_equal, ALU.mult).then_inc(adj_ready, 1)
            V.tensor_reduce(deg[:, :], adj_f.rearrange("p (r n) -> p r n", r=R), AX_X, ALU.add).then_inc(deg_ready, 1)
            dve.wait_ge(deg_ready, 1)
            for r in range(R):
                V.tensor_scalar(deg_b0[:, r, :], b0_rows, deg[:, r:r + 1], None, ALU.mult).then_inc(deg_b0_ready, 1)
            split_weight(0)
            split_weight(1)
            mj_low(0, 0)
            mj_low(0, 1)
            for i in range(2, len(WEIGHTS)):
                split_weight(i)
            dve.wait_ge(deg_b0_ready, R)
            mi_sum(0, 0, first=True)
            mi_sum(0, 1, first=True)
            for r in range(R):
                agg_sum(0, r)
                norm_stats("h", 0, r, read["agg"], h_row)
            norm_mean("h", 0)
            norm_apply("h", 0, h_row)
            hT_low(0, 0)
            hT_low(0, 1)
            dve.wait_ge(bias_loaded, 64)
            q_low(0, 0)
            q_low(0, 1)
            k_low_half(0, 0)
            k_low_half(0, 1)
            v_low(0, 0)
            v_low(0, 1)
            steps(dve, step)
            for r in range(R):
                y_sum(B - 1, r, 1)
                norm_stats("out", B - 1, r, read["y"], hb_row[1])
            norm_mean("out", B - 1)
            norm_apply("out", B - 1, hb_row[1])


def kernel(**inputs):
    import numpy as np
    import concourse.bacc as bacc
    from concourse.bass_utils import run_bass_kernel_spmd

    def array(name):
        return np.asarray(inputs[name])

    def columns(a, p):
        return a.reshape(-1, p).T

    x, adj, w0 = array("x"), array("adj"), array("L0_gnn_W")
    laid_out = {
        "x": x, "xT": x.transpose(0, 2, 1), "adj": adj, "adjT": adj.T,
        "w0T": w0.T, "b0": array("L0_gnn_b"),
        "wqT": array("L1_gnn_Wq").T, "wkT": array("L1_gnn_Wk").T,
        "wvT": array("L1_gnn_Wv").T, "woT": array("L1_gnn_Wo").T,
        "bq": columns(array("L1_gnn_bq"), P), "bk": columns(array("L1_gnn_bk"), P),
        "bv": columns(array("L1_gnn_bv"), P // 2), "bo": array("L1_gnn_bo"),
    }
    nc = bacc.Bacc("TRN2", target_bir_lowering=False, num_devices=1)
    arrays, args = {}, []
    for name, a in laid_out.items():
        a = np.ascontiguousarray(a)
        arrays[f"in_{name}"] = a
        args.append(nc.dram_tensor(f"in_{name}", a.shape, mybir.dt.from_np(a.dtype), kind="ExternalInput").ap())
    args.append(nc.dram_tensor("out_0", x.shape, F32, kind="ExternalOutput").ap())
    build(nc, *args)
    r = run_bass_kernel_spmd(nc, [arrays], core_ids=[0])
    return r.results[0]["out_0"]
```

```python
from contextlib import ExitStack

import concourse.bass as bass
from concourse import mybir

F32 = mybir.dt.float32
F32R = mybir.dt.float32r
I32 = mybir.dt.int32
ALU = mybir.AluOpType
ACT = mybir.ActivationFunctionType
AX_X = mybir.AxisListType.X

P = 128
HEADS = 8
EPS = 1e-5
MASKED = -3.0e38
MAX_FLOOR = -1.0e37
WEIGHTS = ("wj", "wi", "wq", "wk", "wv", "wo")


def build(nc, x, xT, adj, adjT, w0T, b0, wqT, wkT, wvT, woT, bq, bk, bv, bo, out):
    B, N, D = x.shape
    DH = D // HEADS
    R = N // P
    C = D // P
    G = HEADS // 2
    HALF = P // 2
    SCALE = float(DH) ** -0.5
    assert (R, C, G, DH) == (2, 4, 4, HALF) and B % 2 == 0 and B >= 6

    x_rows = x.rearrange("b (r p) d -> b p r d", p=P)
    xT_cols = xT.rearrange("b (c p) n -> b p c n", p=P)
    out_rows = out.rearrange("b (r p) d -> b p r d", p=P)
    w_dram = {
        "wi": w0T[0:D, :], "wj": w0T[D:2 * D, :], "wq": wqT, "wk": wkT, "wv": wvT, "wo": woT,
    }

    with ExitStack() as ctx:
        def sb(name, shape, dt=F32):
            return ctx.enter_context(nc.sbuf_tensor(name, shape, dt))

        def sem(name):
            return ctx.enter_context(nc.semaphore(name))

        def bank(name):
            return ctx.enter_context(nc.psum_tensor(name, [P, 512], F32))

        w_hi = {k: sb(f"{k}_hi", [P, C, D], F32R) for k in WEIGHTS}
        w_lo = {k: sb(f"{k}_lo", [P, C, D], F32R) for k in WEIGHTS}
        aT = sb("aT", [P, R, N], F32R)
        mask_add = sb("mask_add", [P, R, N])
        deg = sb("deg", [P, R])
        deg_b0 = sb("deg_b0", [P, R, D])
        bo_rows = sb("bo_rows", [P, D])
        ident = sb("ident", [P, P])
        eps_cols = sb("eps_cols", [P, R])
        power_cols = sb("power_cols", [P, R])
        zero = sb("zero", [P, 1])
        bq_cols = sb("bq_cols", [P, C])
        bk_cols = sb("bk_cols", [P, C])
        bv_cols = sb("bv_cols", [HALF, HEADS])

        xT_raw = sb("xT_raw", [P, C, N])
        xT_hi = sb("xT_hi", [P, C, N], F32R)
        xT_lo = sb("xT_lo", [P, C, N], F32R)
        xb = sb("xb", [P, R, D])
        mj_hi = sb("mj_hi", [P, R, D], F32R)
        mj_lo = sb("mj_lo", [P, R, D], F32R)
        h = sb("h", [P, R, D])
        hb = sb("hb", [P, 2, R, D])
        hT_hi = sb("hT_hi", [P, C, N], F32R)
        hT_lo = sb("hT_lo", [P, C, N], F32R)
        q_both = sb("q_both", [P, HEADS, N], F32R)
        k_twice = sb("k_twice", [P, HEADS, N], F32R)
        k_lo = sb("k_lo", [P, C, N], F32R)
        v_both = sb("v_both", [P, R, HEADS, 2 * DH], F32R)
        probs = sb("probs", [P, 2, 2, R, N])
        pT_hi = sb("pT_hi", [P, 2, R, N], F32R)
        pT_lo = sb("pT_lo", [P, 2, R, N], F32R)
        o_part = sb("o_part", [HALF, 2, N])
        oT = sb("oT", [P, N])
        oT_hi = sb("oT_hi", [P, G, N], F32R)
        oT_lo = sb("oT_lo", [P, G, N], F32R)
        row_max = sb("row_max", [P, 2, 2 * R])
        exp_bias = sb("exp_bias", [P, 2, 2 * R])
        row_sum = sb("row_sum", [P, 2, 2 * R])
        row_inv = sb("row_inv", [P, 2, 2 * R])
        stats = {k: sb(f"stats_{k}", [P, R, 6]) for k in ("h", "out")}
        mean_var = {k: sb(f"mean_var_{k}", [P, R, 2]) for k in ("h", "out")}
        var_eps = {k: sb(f"var_eps_{k}", [P, R]) for k in ("h", "out")}
        rstd = {k: sb(f"rstd_{k}", [P, R]) for k in ("h", "out")}

        stage = [probs[:, :, :, :, :].rearrange("p a b c d -> p (a b c d)"),
                 hb[:, :, :, :].rearrange("p a b c -> p (a b c)")]
        stage_of = lambda i: stage[i % 2].rearrange("p (c o) -> p c o", c=C)
        adj_i = xb[:, 0, :].bitcast(I32)
        adjT_i = xb[:, 1, :].bitcast(I32)
        adj_f = h[:, 0, :]
        b0_rows = h[:, 1, :]

        proj = [bank(f"proj{i}") for i in range(3)]
        score = [bank(f"score{i}") for i in range(2)]
        pt = [bank(f"pt{i}") for i in range(2)]
        av = bank("av")
        BANK = {"mj": (0, 1), "mi": (2, 0), "agg": (1, 2), "y": (0, 1), "hT": (2, 0),
                "q": (1, 2), "k": (0, 1), "v": (2, 1)}

        w_loaded = {k: sem(f"{k}_loaded") for k in WEIGHTS}
        w_hi_done, w_split = sem("w_hi_done"), sem("w_split")
        const_loaded, bias_loaded = sem("const_loaded"), sem("bias_loaded")
        zeroed, ident_ready = sem("zeroed"), sem("ident_ready")
        adj_ready, deg_ready, deg_b0_ready = sem("adj_ready"), sem("deg_ready"), sem("deg_b0_ready")
        xT_loaded, x_loaded, out_stored = sem("xT_loaded"), sem("x_loaded"), sem("out_stored")
        k_copied = [sem("k_copied0"), sem("k_copied1")]
        norm_odd_done = sem("norm_odd_done")
        xT_hi_done, xT_split = sem("xT_hi_done"), sem("xT_split")
        xb_ready, hb_ready, o_split = sem("xb_ready"), sem("hb_ready"), sem("o_split")
        done = {k: sem(f"{k}_done") for k in BANK}
        score_done, pt_done, av_done = sem("score_done"), sem("pt_done"), sem("av_done")
        hi = {k: sem(f"{k}_hi_done") for k in ("mj", "hT", "q", "k", "v")}
        exp_done, norm_even_done, pt_hi_done = sem("exp_done"), sem("norm_done"), sem("pt_hi_done")
        o_part_done, o_hi_done = sem("o_part_done"), sem("o_hi_done")
        read = {k: sem(f"{k}_read") for k in BANK}
        max_done, bias_done, inv_done = sem("max_done"), sem("bias_done"), sem("inv_done")
        pt_read, av_read = sem("pt_read"), sem("av_read")
        stats_done = {k: sem(f"stats_{k}_done") for k in ("h", "out")}
        aggr_done = {k: sem(f"aggr_{k}_done") for k in ("h", "out")}
        var_eps_done = {k: sem(f"var_eps_{k}_done") for k in ("h", "out")}
        rstd_done = {k: sem(f"rstd_{k}_done") for k in ("h", "out")}
        normed = {k: sem(f"normed_{k}") for k in ("h", "out")}

        def steps(eng, step):
            step(0, parity=0, y_=False)
            with eng.Fori(0, (B - 4) // 2) as i:
                step(2 * i + 1, parity=1)
                step(2 * i + 2, parity=0)
            step(B - 3, parity=1)
            step(B - 2, parity=0, ahead=False)
            step(B - 1, parity=1, ahead=False, proj=False)

        block = ctx.enter_context(nc.Block())

        @block.sync
        def _(sp):
            def load_xT(n):
                sp.dma_start(xT_raw[:, :, :], xT_cols[n, :, :, :]).then_inc(xT_loaded, 16)

            def load_x(n):
                sp.dma_start(xb[:, :, :], x_rows[n, :, :, :]).then_inc(x_loaded, 16)

            def store(b, parity):
                sp.wait_ge(normed["out"], R * (b + 1))
                sp.dma_start(out_rows[b, :, :, :], hb[:, parity, :, :]).then_inc(out_stored, 16)

            def copy_k(n, half):
                sp.wait_ge(hi["k"], 2 * n + half + 1)
                for i in range(2):
                    heads = slice(4 * half + i, 4 * half + i + 3, 2)
                    sp.dma_start(k_twice[(1 - i) * HALF:(2 - i) * HALF, heads, :].bitcast(F32),
                                 k_twice[i * HALF:(i + 1) * HALF, heads, :].bitcast(F32)).then_inc(k_copied[half], 16)

            def step(b, parity, y_=True, ahead=True, proj=True):
                if ahead:
                    sp.wait_ge(xT_split, b + 2)
                    load_xT(b + 2)
                if proj:
                    sp.wait_ge(read["mi"], R * (b + 1))
                    load_x(b + 1)
                if proj:
                    copy_k(b + 1, 0)
                    copy_k(b + 1, 1)
                if y_:
                    store(b - 1, 1 - parity)

            def load_weight(i):
                if i >= 2:
                    sp.wait_ge(w_split, i - 1)
                sp.dma_start(stage_of(i), w_dram[WEIGHTS[i]].rearrange("(c p) o -> p c o",
                                                                       p=P)).then_inc(w_loaded[WEIGHTS[i]], 16)

            load_xT(0)
            load_weight(0)
            load_weight(1)
            sp.dma_start(adjT_i.rearrange("p (r n) -> p r n", r=R),
                         adjT.rearrange("(r p) n -> p r n", p=P)).then_inc(const_loaded, 16)
            sp.dma_start(adj_i.rearrange("p (r n) -> p r n", r=R),
                         adj.rearrange("(r p) n -> p r n", p=P)).then_inc(const_loaded, 16)
            sp.dma_start(b0_rows, b0.partition_broadcast(P)).then_inc(const_loaded, 16)
            sp.wait_ge(xT_split, 1)
            load_xT(1)
            load_weight(2)
            load_weight(3)
            sp.wait_ge(adj_ready, 3)
            load_x(0)
            sp.dma_start(bo_rows[:, :], bo.partition_broadcast(P)).then_inc(bias_loaded, 16)
            sp.dma_start(bq_cols[:, :], bq).then_inc(bias_loaded, 16)
            sp.dma_start(bk_cols[:, :], bk).then_inc(bias_loaded, 16)
            sp.dma_start(bv_cols[:, :], bv).then_inc(bias_loaded, 16)
            load_weight(4)
            load_weight(5)
            copy_k(0, 0)
            copy_k(0, 1)
            steps(sp, step)
            store(B - 1, (B - 1) % 2)
            sp.wait_ge(out_stored, 16 * B)

        @block.gpsimd
        def _(pool):
            def xT_high(n):
                pool.wait_ge(xT_loaded, 16 * (n + 1))
                if type(n) is not int or n > 0:
                    pool.wait_ge(done["mi"], R * n)
                pool.tensor_tensor(xT_hi[:, :, :].rearrange("p c n -> p (c n)"),
                                   xT_raw[:, :, :].rearrange("p c n -> p (c n)"),
                                   zero[:, :].to_broadcast([P, C * N]), ALU.add).then_inc(xT_hi_done, 1)

            def normalise_odd(b, g):
                pool.wait_ge(inv_done, G * b + g + 1)
                pool.tensor_tensor(probs[:, g % 2, 1, :, :], probs[:, g % 2, 1, :, :],
                                   row_inv[:, g % 2, R:2 * R].unsqueeze(2).to_broadcast([P, R, N]),
                                   ALU.mult).then_inc(norm_odd_done, 1)

            def split_xT(n):
                pool.wait_ge(xT_hi_done, n + 1)
                pool.tensor_tensor(xT_lo[:, :, :], xT_raw[:, :, :], xT_hi[:, :, :].bitcast(F32),
                                   ALU.subtract).then_inc(xT_split, 1)

            def add_bias(n):
                pool.wait_ge(x_loaded, 16 * (n + 1))
                pool.tensor_tensor(xb[:, :, :], xb[:, :, :], deg_b0[:, :, :], ALU.add).then_inc(xb_ready, 1)

            def residual(n, parity, stored):
                pool.wait_ge(normed["h"], R * (n + 1))
                if stored:
                    pool.wait_ge(out_stored, 16 * (n - 1))
                for r in range(R):
                    last = pool.tensor_tensor(hb[:, parity, r, :], h[:, r, :], bo_rows[:, :], ALU.add)
                last.then_inc(hb_ready, 1)

            def root(which, n):
                pool.wait_ge(aggr_done[which], R * n + R)
                pool.tensor_tensor(var_eps[which][:, :], mean_var[which][:, :, 1], eps_cols[:, :],
                                   ALU.add).then_inc(var_eps_done[which], 1)
                pool.wait_ge(var_eps_done[which], n + 1)
                pool.tensor_tensor(rstd[which][:, :], var_eps[which][:, :], power_cols[:, :],
                                   ALU.pow).then_inc(rstd_done[which], 1)

            def split_o(b, g):
                pool.wait_ge(o_hi_done, G * b + g + 1)
                pool.tensor_tensor(oT_lo[:, g, :], oT[:, :], oT_hi[:, g, :].bitcast(F32),
                                   ALU.subtract).then_inc(o_split, 1)

            pool.memset(ident[:, :], 0.0).then_inc(zeroed, 1)
            pool.wait_ge(zeroed, 1)
            pool.affine_select(out=ident[:, :], in_=ident[:, :], compare_op=ALU.not_equal, fill=1.0, base=0,
                               pattern=[[-1, P]], channel_multiplier=1).then_inc(ident_ready, 1)
            pool.memset(eps_cols[:, :], EPS).then_inc(zeroed, 1)
            pool.memset(power_cols[:, :], -0.5).then_inc(zeroed, 1)
            pool.memset(zero[:, :], 0.0).then_inc(zeroed, 1)
            pool.wait_ge(zeroed, 4)
            xT_high(0)
            split_xT(0)
            pool.wait_ge(deg_b0_ready, R)
            add_bias(0)
            root("h", 0)
            xT_high(1)
            split_xT(1)
            pool.wait_ge(bias_loaded, 64)
            pool.wait_ge(w_split, len(WEIGHTS))
            residual(0, 0, stored=False)

            def step(b, parity, y_=True, ahead=True, proj=True):
                n = b + 1
                if proj: add_bias(n)
                normalise_odd(b, 0)
                if proj: root("h", n)
                normalise_odd(b, 1)
                normalise_odd(b, 2)
                normalise_odd(b, 3)
                split_o(b, 0)
                if ahead: xT_high(b + 2)
                split_o(b, 1)
                if ahead: split_xT(b + 2)
                if y_: root("out", b - 1)
                split_o(b, 2)
                if proj: residual(n, 1 - parity, stored=y_)
                split_o(b, 3)

            steps(pool, step)
            root("out", B - 1)

        @block.tensor
        def _(pe):
            def mm(dst, lhsT, rhs, start, stop):
                return pe.matmul(dst, lhsT, rhs, start=start, stop=stop)

            def product(dst, l_hi, l_lo, r_hi, r_lo):
                terms = [(a(c), b(c)) for c in range(C) for a, b in ((l_hi, r_hi), (l_lo, r_hi), (l_hi, r_lo))]
                for i, (a, b) in enumerate(terms):
                    last = mm(dst, a, b, i == 0, i == len(terms) - 1)
                return last

            def rows_times_w(kind, r, l_hi, l_lo, w):
                rows = slice(r * P, (r + 1) * P)
                product(proj[BANK[kind][r]][:, :], lambda c: l_hi[:, c, rows], lambda c: l_lo[:, c, rows],
                        lambda c: w_hi[w][:, c, :], lambda c: w_lo[w][:, c, :]).then_inc(done[kind], 1)

            def mj(n, r, first=False):
                if r == 0:
                    pe.wait_ge(xT_split, n + 1)
                    if first:
                        pe.wait_ge(w_split, 1)
                    else:
                        pe.wait_ge(read["k"], 2 * n - 1)
                elif not first:
                    pe.wait_ge(read["v"], R * n)
                rows_times_w("mj", r, xT_hi, xT_lo, "wj")

            def mi(n, r, first=False):
                if first and r == 0:
                    pe.wait_ge(w_split, 2)
                if r == 1:
                    pe.wait_ge(read["mj"], R * n + 1)
                rows_times_w("mi", r, xT_hi, xT_lo, "wi")

            def aggregate(n, r):
                if r == 0:
                    pe.wait_ge(read["mj"], R * n + 2)
                else:
                    pe.wait_ge(read["mi"], R * n + 1)
                terms = [(aT[:, j, r * P:(r + 1) * P], half[:, j, :]) for j in range(R) for half in (mj_hi, mj_lo)]
                for i, (a, m) in enumerate(terms):
                    last = mm(proj[BANK["agg"][r]][:, :], a, m, i == 0, i == len(terms) - 1)
                last.then_inc(done["agg"], 1)

            def y(b, r, tail=False):
                if r == 0:
                    pe.wait_ge(o_split, G * (b + 1))
                if r == 0 and not tail:
                    pe.wait_ge(read["mi"], R * (b + 3))
                elif r == 1 and not tail:
                    pe.wait_ge(read["agg"], R * (b + 2) + 1)
                rows_times_w("y", r, oT_hi, oT_lo, "wo")

            def transpose_h(n, half, first=False):
                if half == 0:
                    pe.wait_ge(normed["h"], R * (n + 1))
                elif type(n) is not int or n >= 2:
                    pe.wait_ge(read["y"], R * (n - 2) + 1)
                if first:
                    pe.wait_ge(ident_ready, 1)
                dst = proj[BANK["hT"][half]][:, :].rearrange("p (c n) -> p c n", c=2)
                for c in range(2):
                    for r in range(R):
                        last = pe.transpose(dst[:, c, r * P:(r + 1) * P],
                                            h[:, r, (2 * half + c) * P:(2 * half + c + 1) * P], ident[:, :])
                last.then_inc(done["hT"], 1)

            def cols_of(kind, n, half, w):
                dst = proj[BANK[kind][half]][:, :].rearrange("p (c n) -> p c n", c=2)
                for c in range(2):
                    cols = slice((2 * half + c) * P, (2 * half + c + 1) * P)
                    last = product(dst[:, c, :], lambda k: w_hi[w][:, k, cols], lambda k: w_lo[w][:, k, cols],
                                   lambda k: hT_hi[:, k, :], lambda k: hT_lo[:, k, :])
                last.then_inc(done[kind], 1)

            def q(n, half, first=False):
                if first:
                    pe.wait_ge(w_split, 3)
                if half == 0:
                    pe.wait_ge(read["hT"], 2 * n + 2)
                    if type(n) is not int or n >= 2:
                        pe.wait_ge(read["y"], R * (n - 1))
                cols_of("q", n, half, "wq")

            def k(n, half, first=False):
                if first:
                    pe.wait_ge(w_split, 4)
                if half == 1:
                    pe.wait_ge(read["q"], 2 * n + 1)
                cols_of("k", n, half, "wk")

            def v(n, r, first=False):
                if first:
                    pe.wait_ge(w_split, 5)
                if r == 0:
                    pe.wait_ge(read["q"], 2 * n + 2)
                else:
                    pe.wait_ge(read["k"], 2 * n + 2)
                rows_times_w("v", r, hT_hi, hT_lo, "wv")

            def scores(b, g, first=False):
                pe.wait_ge(read["q"], 2 * b + g // 2 + 1)
                pe.wait_ge(read["k"], 2 * b + g // 2 + 1)
                pe.wait_ge(k_copied[g // 2], 32 * (b + 1))
                if not (first and g == 0):
                    pe.wait_ge(max_done, 2 * (G * b + g))
                blocks = [(i, r) for i in range(2) for r in range(R)]
                for i, r in blocks:
                    head = 2 * g + i
                    pe.matmul(score[i][:, r * N:(r + 1) * N], q_both[:, head, r * P:(r + 1) * P],
                              k_twice[:, head, :], start=(r == 0), stop=False, skip_group_check=True)
                for i, r in blocks:
                    head, home = 2 * g + i, slice(i * HALF, (i + 1) * HALF)
                    last = pe.matmul(score[i][:, r * N:(r + 1) * N], q_both[home, head, r * P:(r + 1) * P],
                                     k_lo[home, g, :], start=False, stop=True, skip_group_check=True)
                    if r == R - 1:
                        last.then_inc(score_done, 1)

            def transpose_p(b, g, i, first=False):
                pe.wait_ge((norm_even_done, norm_odd_done)[i], G * b + g + 1)
                if not (first and g == 0):
                    pe.wait_ge(pt_read, 2 * (G * b + g) + i - 1)
                dst = pt[i][:, :].rearrange("p (k q) -> p k q", k=R)
                for kt in range(R):
                    for r in range(R):
                        last = pe.transpose(dst[:, kt, r * P:(r + 1) * P],
                                            probs[:, g % 2, i, r, kt * P:(kt + 1) * P], ident[:, :])
                last.then_inc(pt_done, 1)

            def attend(b, g, first=False):
                if g == 0:
                    pe.wait_ge(read["v"], R * (b + 1))
                pe.wait_ge(pt_read, 2 * (G * b + g) + 2)
                if not (first and g == 0):
                    pe.wait_ge(av_read, G * b + g)
                for i in range(2):
                    terms = [(kt, half) for kt in range(R) for half in (pT_hi, pT_lo)]
                    for j, (kt, half) in enumerate(terms):
                        last = mm(av[:, i * N:(i + 1) * N], v_both[:, kt, 2 * g + i, :], half[:, i, kt, :],
                                  j == 0, j == len(terms) - 1)
                last.then_inc(av_done, 1)

            def step(b, parity, y_=True, ahead=True, proj=True):
                n = b + 1
                if proj: mj(n, 0)
                scores(b, 0, not y_)
                if proj: mj(n, 1)
                scores(b, 1)
                if proj: mi(n, 0)
                if proj: mi(n, 1)
                if proj: aggregate(n, 0)
                scores(b, 2)
                transpose_p(b, 0, 0, not y_)
                if proj: aggregate(n, 1)
                transpose_p(b, 0, 1, not y_)
                if y_: y(b - 1, 0, not proj)
                if y_: y(b - 1, 1, not proj)
                if proj: transpose_h(n, 0)
                if proj: transpose_h(n, 1)
                scores(b, 3)
                transpose_p(b, 1, 0)
                transpose_p(b, 1, 1)
                attend(b, 0, not y_)
                if proj: q(n, 0)
                transpose_p(b, 2, 0)
                if proj: q(n, 1)
                attend(b, 1)
                if proj: k(n, 0)
                transpose_p(b, 2, 1)
                if proj: k(n, 1)
                if proj: v(n, 0)
                attend(b, 2)
                transpose_p(b, 3, 0)
                transpose_p(b, 3, 1)
                if proj: v(n, 1)
                attend(b, 3)

            for r in range(R):
                mj(0, r, first=True)
            for r in range(R):
                mi(0, r, first=True)
            pe.wait_ge(adj_ready, 1)
            for r in range(R):
                aggregate(0, r)
            for half in range(2):
                transpose_h(0, half, first=True)
            for half in range(2):
                q(0, half, first=True)
            for half in range(2):
                k(0, half, first=True)
            for r in range(R):
                v(0, r, first=True)
            pe.wait_ge(w_split, len(WEIGHTS))
            steps(pe, step)
            for r in range(R):
                y(B - 1, r, tail=True)

        @block.scalar
        def _(act):
            def copy_hi(kind, n, tile, dst, src):
                act.wait_ge(done[kind], 2 * n + tile + 1)
                nc.scalar.copy(dst, src).then_inc(hi[kind], 1)

            def mj_high(n, r):
                copy_hi("mj", n, r, mj_hi[:, r, :], proj[BANK["mj"][r]][:, :])

            def hT_high(n, half):
                copy_hi("hT", n, half, hT_hi[:, 2 * half:2 * half + 2, :],
                        proj[BANK["hT"][half]][:, :].rearrange("p (c n) -> p c n", c=2))

            def v_high(n, r):
                if r == 0 and not (type(n) is int and n == 0):
                    act.wait_ge(av_done, G * n)
                copy_hi("v", n, r, v_both[:, r, :, 0:DH],
                        proj[BANK["v"][r]][:, :].rearrange("p (h d) -> p h d", h=HEADS))

            def heads_used(n, half):
                if not (type(n) is int and n == 0):
                    act.wait_ge(score_done, 2 * G * (n - 1) + G * (half + 1))

            def q_high(n, half):
                heads_used(n, half)
                act.wait_ge(done["q"], 2 * n + half + 1)
                for c in range(2):
                    t = 2 * half + c
                    src = proj[BANK["q"][half]][:, c * N:(c + 1) * N]
                    for i in range(2):
                        home = slice(i * HALF, (i + 1) * HALF)
                        last = nc.scalar.activation(q_both[home, 2 * t + i, :], src[home, :], ACT.Identity,
                                                    bias=bq_cols[home, t:t + 1])
                last.then_inc(hi["q"], 1)

            def k_high(n, half):
                heads_used(n, half)
                act.wait_ge(done["k"], 2 * n + half + 1)
                for c in range(2):
                    t = 2 * half + c
                    src = proj[BANK["k"][half]][:, c * N:(c + 1) * N]
                    for i in range(2):
                        home = slice(i * HALF, (i + 1) * HALF)
                        last = nc.scalar.activation(k_twice[home, 2 * t + i, :], src[home, :], ACT.Identity,
                                                    bias=bk_cols[home, t:t + 1])
                last.then_inc(hi["k"], 1)

            def exponentials(b, g):
                act.wait_ge(bias_done, G * b + g + 1)
                for i in range(2):
                    for r in range(R):
                        s = R * i + r
                        e = probs[:, g % 2, i, r, :]
                        last = nc.scalar.activation(e, e, ACT.Exp, bias=exp_bias[:, g % 2, s:s + 1], scale=SCALE,
                                                    accum_out=row_sum[:, g % 2, s:s + 1])
                last.then_inc(exp_done, 1)

            def normalise_even(b, g):
                act.wait_ge(inv_done, G * b + g + 1)
                for r in range(R):
                    e = probs[:, g % 2, 0, r, :]
                    last = nc.scalar.activation(e, e, ACT.Copy, scale=row_inv[:, g % 2, r:r + 1])
                last.then_inc(norm_even_done, 1)

            def pt_high(b, g, i, first=False):
                act.wait_ge(pt_done, 2 * (G * b + g) + i + 1)
                if i == 0 and not (first and g == 0):
                    act.wait_ge(av_done, G * b + g)
                nc.scalar.copy(pT_hi[:, i, :, :],
                               pt[i][:, :].rearrange("p (k q) -> p k q", k=R)).then_inc(pt_hi_done, 1)

            def o_low_part(b, g, first=False):
                act.wait_ge(av_done, G * b + g + 1)
                if not (first and g == 0):
                    act.wait_ge(av_read, G * b + g)
                nc.scalar.copy(o_part[:, :, :],
                               av[HALF:P, :].rearrange("p (i n) -> p i n", i=2)).then_inc(o_part_done, 1)

            def o_high(b, g, first=False):
                act.wait_ge(av_read, G * b + g + 1)
                if g == 0 and not first:
                    act.wait_ge(done["y"], R * b)
                nc.scalar.copy(oT_hi[:, g, :], oT[:, :]).then_inc(o_hi_done, 1)

            def step(b, parity, y_=True, ahead=True, proj=True):
                n = b + 1
                if proj: mj_high(n, 0)
                if proj: mj_high(n, 1)
                exponentials(b, 0)
                normalise_even(b, 0)
                pt_high(b, 0, 0, not y_)
                pt_high(b, 0, 1, not y_)
                exponentials(b, 1)
                exponentials(b, 2)
                normalise_even(b, 1)
                if proj: hT_high(n, 0)
                if proj: hT_high(n, 1)
                pt_high(b, 1, 0)
                pt_high(b, 1, 1)
                normalise_even(b, 2)
                o_low_part(b, 0, not y_)
                exponentials(b, 3)
                o_high(b, 0, not y_)
                if proj: q_high(n, 0)
                if proj: q_high(n, 1)
                o_low_part(b, 1)
                o_high(b, 1)
                pt_high(b, 2, 0)
                if proj: k_high(n, 0)
                normalise_even(b, 3)
                pt_high(b, 2, 1)
                if proj: k_high(n, 1)
                o_low_part(b, 2)
                pt_high(b, 3, 0)
                pt_high(b, 3, 1)
                o_low_part(b, 3)
                o_high(b, 2)
                if proj: v_high(n, 0)
                if proj: v_high(n, 1)
                o_high(b, 3)

            def split_weight(i):
                act.wait_ge(w_loaded[WEIGHTS[i]], 16)
                nc.scalar.copy(w_hi[WEIGHTS[i]][:, :, :], stage_of(i)).then_inc(w_hi_done, 1)

            split_weight(0)
            split_weight(1)
            mj_high(0, 0)
            mj_high(0, 1)
            for i in range(2, 5):
                split_weight(i)
            hT_high(0, 0)
            hT_high(0, 1)
            act.wait_ge(bias_loaded, 64)
            q_high(0, 0)
            q_high(0, 1)
            split_weight(5)
            k_high(0, 0)
            k_high(0, 1)
            v_high(0, 0)
            v_high(0, 1)
            steps(act, step)

        @block.vector
        def _(dve):
            V = nc.vector

            def low(kind, n, tile, dst, src, high):
                dve.wait_ge(hi[kind], 2 * n + tile + 1)
                V.tensor_tensor(dst, src, high.bitcast(F32), ALU.subtract).then_inc(read[kind], 1)

            def mj_low(n, r):
                low("mj", n, r, mj_lo[:, r, :], proj[BANK["mj"][r]][:, :], mj_hi[:, r, :])

            def hT_low(n, half):
                cs = slice(2 * half, 2 * half + 2)
                low("hT", n, half, hT_lo[:, cs, :],
                    proj[BANK["hT"][half]][:, :].rearrange("p (c n) -> p c n", c=2), hT_hi[:, cs, :])

            def v_low(n, r):
                low("v", n, r, v_both[:, r, :, DH:2 * DH],
                    proj[BANK["v"][r]][:, :].rearrange("p (h d) -> p h d", h=HEADS), v_both[:, r, :, 0:DH])

            def biased_low(kind, n, half, bias, high, dst):
                dve.wait_ge(hi[kind], 2 * n + half + 1)
                for c in range(2):
                    t = 2 * half + c
                    src = proj[BANK[kind][half]][:, c * N:(c + 1) * N]
                    for i in range(2):
                        home = slice(i * HALF, (i + 1) * HALF)
                        last = V.scalar_tensor_tensor(
                            out=dst(t, i), in0=src[home, :], scalar=bias[home, t:t + 1],
                            in1=high[home, 2 * t + i, :].bitcast(F32), op0=ALU.add, op1=ALU.subtract)
                last.then_inc(read[kind], 1)

            def q_low(n, half):
                biased_low("q", n, half, bq_cols, q_both,
                           lambda t, i: q_both[(1 - i) * HALF:(2 - i) * HALF, 2 * t + i, :])

            def k_low_half(n, half):
                biased_low("k", n, half, bk_cols, k_twice,
                           lambda t, i: k_lo[i * HALF:(i + 1) * HALF, t, :])

            def maxima(b, g, first=False):
                for i in range(2):
                    dve.wait_ge(score_done, 2 * (G * b + g) + i + 1)
                    if i == 0 and not (first and g < 2):
                        dve.wait_ge(pt_done, 2 * (G * b + g) - 2)
                    dve.nop(nofuse=True)
                    for r in range(R):
                        s = R * i + r
                        last = V.tensor_tensor_reduce(
                            out=probs[:, g % 2, i, r, :], in0=score[i][:, r * N:(r + 1) * N],
                            in1=mask_add[:, r, :], scale=1.0, scalar=MASKED, op0=ALU.add, op1=ALU.max,
                            accum_out=row_max[:, g % 2, s:s + 1])
                    last.then_inc(max_done, 1)
                dve.wait_ge(max_done, 2 * (G * b + g) + 2)
                V.tensor_scalar(exp_bias[:, g % 2, :], row_max[:, g % 2, :], MAX_FLOOR, -SCALE,
                                ALU.max, ALU.mult).then_inc(bias_done, 1)

            def inverse_sums(b, g):
                dve.wait_ge(exp_done, G * b + g + 1)
                V.reciprocal(row_inv[:, g % 2, :], row_sum[:, g % 2, :]).then_inc(inv_done, 1)

            def pt_low(b, g, i):
                dve.wait_ge(pt_hi_done, 2 * (G * b + g) + i + 1)
                V.tensor_tensor(pT_lo[:, i, :, :], pt[i][:, :].rearrange("p (k q) -> p k q", k=R),
                                pT_hi[:, i, :, :].bitcast(F32), ALU.subtract).then_inc(pt_read, 1)

            def o_sum(b, g, first=False):
                dve.wait_ge(o_part_done, G * b + g + 1)
                if not (first and g == 0):
                    dve.wait_ge(o_split, G * b + g)
                for i in range(2):
                    last = V.scalar_tensor_tensor(
                        out=oT[i * HALF:(i + 1) * HALF, :], in0=av[0:HALF, i * N:(i + 1) * N],
                        scalar=bv_cols[:, 2 * g + i:2 * g + i + 1], in1=o_part[:, i, :],
                        op0=ALU.add, op1=ALU.add)
                last.then_inc(av_read, 1)

            def mi_sum(n, r, first=False):
                dve.wait_ge(done["mi"], R * n + r + 1)
                dve.wait_ge(xb_ready, n + 1)
                if not first:
                    dve.wait_ge(hb_ready, n)
                V.scalar_tensor_tensor(out=h[:, r, :], in0=proj[BANK["mi"][r]][:, :], scalar=deg[:, r:r + 1],
                                       in1=xb[:, r, :], op0=ALU.mult, op1=ALU.add).then_inc(read["mi"], 1)

            def agg_sum(n, r):
                dve.wait_ge(done["agg"], R * n + r + 1)
                dve.wait_ge(read["mi"], R * n + r + 1)
                V.tensor_tensor(h[:, r, :], proj[BANK["agg"][r]][:, :], h[:, r, :],
                                ALU.add).then_inc(read["agg"], 1)

            def y_sum(b, r, parity):
                dve.wait_ge(done["y"], R * b + r + 1)
                dve.wait_ge(hb_ready, b + 1)
                V.tensor_tensor(hb[:, parity, r, :], proj[BANK["y"][r]][:, :], hb[:, parity, r, :],
                                ALU.add).then_inc(read["y"], 1)

            h_row = lambda r: h[:, r, :]
            hb_row = [lambda r: hb[:, 0, r, :], lambda r: hb[:, 1, r, :]]

            def norm_stats(which, n, r, summed, row):
                dve.wait_ge(summed, R * n + r + 1)
                V.bn_stats(stats[which][:, r, :], row(r)).then_inc(stats_done[which], 1)

            def norm_mean(which, n):
                dve.wait_ge(stats_done[which], R * n + R)
                dve.nop(nofuse=True)
                for r in range(R):
                    V.bn_aggr(mean_var[which][:, r, :], stats[which][:, r, :]).then_inc(aggr_done[which], 1)

            def norm_apply(which, n, row):
                dve.wait_ge(rstd_done[which], n + 1)
                for r in range(R):
                    V.tensor_scalar(row(r), row(r), mean_var[which][:, r, 0:1], rstd[which][:, r:r + 1],
                                    ALU.subtract, ALU.mult).then_inc(normed[which], 1)

            def step(b, parity, y_=True, ahead=True, proj=True):
                n, other = b + 1, 1 - parity
                maxima(b, 0, not y_)
                if proj: mj_low(n, 0)
                if proj: mj_low(n, 1)
                if proj: mi_sum(n, 0)
                inverse_sums(b, 0)
                maxima(b, 1, not y_)
                if proj: mi_sum(n, 1)
                if proj: agg_sum(n, 0)
                if proj: norm_stats("h", n, 0, read["agg"], h_row)
                pt_low(b, 0, 0)
                if proj: agg_sum(n, 1)
                if proj: norm_stats("h", n, 1, read["agg"], h_row)
                if proj: norm_mean("h", n)
                maxima(b, 2)
                if proj: norm_apply("h", n, h_row)
                if y_: y_sum(b - 1, 0, other)
                inverse_sums(b, 1)
                pt_low(b, 0, 1)
                if y_: y_sum(b - 1, 1, other)
                inverse_sums(b, 2)
                if proj: hT_low(n, 0)
                if proj: hT_low(n, 1)
                maxima(b, 3)
                pt_low(b, 1, 0)
                if y_: norm_stats("out", b - 1, 0, read["y"], hb_row[other])
                if y_: norm_stats("out", b - 1, 1, read["y"], hb_row[other])
                o_sum(b, 0, not y_)
                pt_low(b, 1, 1)
                inverse_sums(b, 3)
                if proj: q_low(n, 0)
                o_sum(b, 1)
                if proj: q_low(n, 1)
                if y_: norm_mean("out", b - 1)
                pt_low(b, 2, 0)
                if proj: k_low_half(n, 0)
                pt_low(b, 2, 1)
                if proj: k_low_half(n, 1)
                o_sum(b, 2)
                pt_low(b, 3, 0)
                pt_low(b, 3, 1)
                if y_: norm_apply("out", b - 1, hb_row[other])
                if proj: v_low(n, 0)
                if proj: v_low(n, 1)
                o_sum(b, 3)

            def split_weight(i):
                dve.wait_ge(w_hi_done, i + 1)
                V.tensor_tensor(w_lo[WEIGHTS[i]][:, :, :], stage_of(i), w_hi[WEIGHTS[i]][:, :, :].bitcast(F32),
                                ALU.subtract).then_inc(w_split, 1)

            split_weight(0)
            split_weight(1)
            dve.wait_ge(const_loaded, 48)
            V.tensor_copy(aT[:, :, :], adjT_i.rearrange("p (r n) -> p r n", r=R)).then_inc(adj_ready, 1)
            V.tensor_copy(adj_f, adj_i).then_inc(adj_ready, 1)
            dve.wait_ge(adj_ready, 2)
            V.tensor_scalar(mask_add[:, :, :], adj_f.rearrange("p (r n) -> p r n", r=R), 0.0, MASKED,
                            ALU.is_equal, ALU.mult).then_inc(adj_ready, 1)
            V.tensor_reduce(deg[:, :], adj_f.rearrange("p (r n) -> p r n", r=R), AX_X, ALU.add).then_inc(deg_ready, 1)
            dve.wait_ge(deg_ready, 1)
            for r in range(R):
                V.tensor_scalar(deg_b0[:, r, :], b0_rows, deg[:, r:r + 1], None, ALU.mult).then_inc(deg_b0_ready, 1)
            mj_low(0, 0)
            mj_low(0, 1)
            split_weight(2)
            dve.wait_ge(deg_b0_ready, R)
            mi_sum(0, 0, first=True)
            mi_sum(0, 1, first=True)
            for r in range(R):
                agg_sum(0, r)
                norm_stats("h", 0, r, read["agg"], h_row)
            norm_mean("h", 0)
            split_weight(3)
            norm_apply("h", 0, h_row)
            hT_low(0, 0)
            hT_low(0, 1)
            split_weight(4)
            dve.wait_ge(bias_loaded, 64)
            q_low(0, 0)
            q_low(0, 1)
            split_weight(5)
            k_low_half(0, 0)
            k_low_half(0, 1)
            v_low(0, 0)
            v_low(0, 1)
            steps(dve, step)
            for r in range(R):
                y_sum(B - 1, r, 1)
                norm_stats("out", B - 1, r, read["y"], hb_row[1])
            norm_mean("out", B - 1)
            norm_apply("out", B - 1, hb_row[1])


def kernel(**inputs):
    import numpy as np
    import concourse.bacc as bacc
    from concourse.bass_utils import run_bass_kernel_spmd

    def array(name):
        return np.asarray(inputs[name])

    def columns(a, p):
        return a.reshape(-1, p).T

    x, adj, w0 = array("x"), array("adj"), array("L0_gnn_W")
    laid_out = {
        "x": x, "xT": x.transpose(0, 2, 1), "adj": adj, "adjT": adj.T,
        "w0T": w0.T, "b0": array("L0_gnn_b"),
        "wqT": array("L1_gnn_Wq").T, "wkT": array("L1_gnn_Wk").T,
        "wvT": array("L1_gnn_Wv").T, "woT": array("L1_gnn_Wo").T,
        "bq": columns(array("L1_gnn_bq"), P), "bk": columns(array("L1_gnn_bk"), P),
        "bv": columns(array("L1_gnn_bv"), P // 2), "bo": array("L1_gnn_bo"),
    }
    nc = bacc.Bacc("TRN2", target_bir_lowering=False, num_devices=1)
    arrays, args = {}, []
    for name, a in laid_out.items():
        a = np.ascontiguousarray(a)
        arrays[f"in_{name}"] = a
        args.append(nc.dram_tensor(f"in_{name}", a.shape, mybir.dt.from_np(a.dtype), kind="ExternalInput").ap())
    args.append(nc.dram_tensor("out_0", x.shape, F32, kind="ExternalOutput").ap())
    build(nc, *args)
    r = run_bass_kernel_spmd(nc, [arrays], core_ids=[0])
    return r.results[0]["out_0"]
```

```python
from contextlib import ExitStack

import concourse.bass as bass
from concourse import mybir

F32 = mybir.dt.float32
F32R = mybir.dt.float32r
I32 = mybir.dt.int32
ALU = mybir.AluOpType
ACT = mybir.ActivationFunctionType
AX_X = mybir.AxisListType.X

P = 128
HEADS = 8
EPS = 1e-5
MASKED = -3.0e38
MAX_FLOOR = -1.0e37
WEIGHTS = ("wj", "wi", "wq", "wk", "wv", "wo")


def build(nc, x, xT, adj, adjT, w0T, b0, wqT, wkT, wvT, woT, bq, bk, bv, bo, out):
    B, N, D = x.shape
    DH = D // HEADS
    R = N // P
    C = D // P
    G = HEADS // 2
    HALF = P // 2
    SCALE = float(DH) ** -0.5
    assert (R, C, G, DH) == (2, 4, 4, HALF) and B % 2 == 0 and B >= 6

    x_rows = x.rearrange("b (r p) d -> b p r d", p=P)
    xT_cols = xT.rearrange("b (c p) n -> b p c n", p=P)
    out_rows = out.rearrange("b (r p) d -> b p r d", p=P)
    w_dram = {
        "wi": w0T[0:D, :], "wj": w0T[D:2 * D, :], "wq": wqT, "wk": wkT, "wv": wvT, "wo": woT,
    }

    with ExitStack() as ctx:
        def sb(name, shape, dt=F32):
            return ctx.enter_context(nc.sbuf_tensor(name, shape, dt))

        def sem(name):
            return ctx.enter_context(nc.semaphore(name))

        def bank(name):
            return ctx.enter_context(nc.psum_tensor(name, [P, 512], F32))

        w_hi = {k: sb(f"{k}_hi", [P, C, D], F32R) for k in WEIGHTS}
        w_lo = {k: sb(f"{k}_lo", [P, C, D], F32R) for k in WEIGHTS}
        aT = sb("aT", [P, R, N], F32R)
        mask_add = sb("mask_add", [P, R, N])
        deg = sb("deg", [P, R])
        deg_b0 = sb("deg_b0", [P, R, D])
        bo_rows = sb("bo_rows", [P, D])
        ident = sb("ident", [P, P])
        eps_cols = sb("eps_cols", [P, R])
        power_cols = sb("power_cols", [P, R])
        zero = sb("zero", [P, 1])
        bq_cols = sb("bq_cols", [P, C])
        bk_cols = sb("bk_cols", [P, C])
        bv_cols = sb("bv_cols", [HALF, HEADS])

        xT_raw = sb("xT_raw", [P, C, N])
        xT_hi = sb("xT_hi", [P, C, N], F32R)
        xT_lo = sb("xT_lo", [P, C, N], F32R)
        xb = sb("xb", [P, R, D])
        mj_hi = sb("mj_hi", [P, R, D], F32R)
        mj_lo = sb("mj_lo", [P, R, D], F32R)
        h = sb("h", [P, R, D])
        hb = sb("hb", [P, 2, R, D])
        hT_hi = sb("hT_hi", [P, C, N], F32R)
        hT_lo = sb("hT_lo", [P, C, N], F32R)
        q_both = sb("q_both", [P, HEADS, N], F32R)
        k_twice = sb("k_twice", [P, HEADS, N], F32R)
        k_lo = sb("k_lo", [P, C, N], F32R)
        v_both = sb("v_both", [P, R, HEADS, 2 * DH], F32R)
        probs = sb("probs", [P, 2, 2, R, N])
        pT_hi = sb("pT_hi", [P, 2, R, N], F32R)
        pT_lo = sb("pT_lo", [P, 2, R, N], F32R)
        o_part = sb("o_part", [HALF, 2, N])
        oT = sb("oT", [P, N])
        oT_hi = sb("oT_hi", [P, G, N], F32R)
        oT_lo = sb("oT_lo", [P, G, N], F32R)
        row_max = sb("row_max", [P, 2, 2 * R])
        exp_bias = sb("exp_bias", [P, 2, 2 * R])
        row_sum = sb("row_sum", [P, 2, 2 * R])
        row_inv = sb("row_inv", [P, 2, 2 * R])
        stats = {k: sb(f"stats_{k}", [P, R, 6]) for k in ("h", "out")}
        mean_var = {k: sb(f"mean_var_{k}", [P, R, 2]) for k in ("h", "out")}
        var_eps = {k: sb(f"var_eps_{k}", [P, R]) for k in ("h", "out")}
        rstd = {k: sb(f"rstd_{k}", [P, R]) for k in ("h", "out")}

        stage = [probs[:, :, :, :, :].rearrange("p a b c d -> p (a b c d)"),
                 hb[:, :, :, :].rearrange("p a b c -> p (a b c)")]
        stage_of = lambda i: stage[i % 2].rearrange("p (c o) -> p c o", c=C)
        adj_i = xb[:, 0, :].bitcast(I32)
        adjT_i = xb[:, 1, :].bitcast(I32)
        adj_f = h[:, 0, :]
        b0_rows = h[:, 1, :]

        proj = [bank(f"proj{i}") for i in range(3)]
        score = [bank(f"score{i}") for i in range(2)]
        pt = [bank(f"pt{i}") for i in range(2)]
        av = bank("av")
        BANK = {"mj": (0, 1), "mi": (2, 0), "agg": (1, 2), "y": (0, 1), "hT": (2, 0),
                "q": (1, 2), "k": (0, 1), "v": (2, 1)}

        w_loaded = {k: sem(f"{k}_loaded") for k in WEIGHTS}
        w_hi_done, w_split = sem("w_hi_done"), sem("w_split")
        const_loaded, bias_loaded = sem("const_loaded"), sem("bias_loaded")
        zeroed, ident_ready = sem("zeroed"), sem("ident_ready")
        adj_ready, deg_ready, deg_b0_ready = sem("adj_ready"), sem("deg_ready"), sem("deg_b0_ready")
        xT_loaded, x_loaded, out_stored = sem("xT_loaded"), sem("x_loaded"), sem("out_stored")
        k_copied = [sem("k_copied0"), sem("k_copied1")]
        norm_odd_done = sem("norm_odd_done")
        xT_hi_done, xT_split = sem("xT_hi_done"), sem("xT_split")
        xb_ready, hb_ready, o_split = sem("xb_ready"), sem("hb_ready"), sem("o_split")
        done = {k: sem(f"{k}_done") for k in BANK}
        score_done, pt_done, av_done = sem("score_done"), sem("pt_done"), sem("av_done")
        hi = {k: sem(f"{k}_hi_done") for k in ("mj", "hT", "q", "k", "v")}
        exp_done, norm_even_done, pt_hi_done = sem("exp_done"), sem("norm_even_done"), sem("pt_hi_done")
        o_part_done, o_hi_done = sem("o_part_done"), sem("o_hi_done")
        read = {k: sem(f"{k}_read") for k in BANK}
        max_done, bias_done, inv_done = sem("max_done"), sem("bias_done"), sem("inv_done")
        pt_read, av_read = sem("pt_read"), sem("av_read")
        stats_done = {k: sem(f"stats_{k}_done") for k in ("h", "out")}
        aggr_done = {k: sem(f"aggr_{k}_done") for k in ("h", "out")}
        var_eps_done = {k: sem(f"var_eps_{k}_done") for k in ("h", "out")}
        rstd_done = {k: sem(f"rstd_{k}_done") for k in ("h", "out")}
        normed = {k: sem(f"normed_{k}") for k in ("h", "out")}

        def steps(eng, step, last_step):
            step(0, parity=0, y_=False)
            with eng.Fori(0, (B - 4) // 2) as i:
                step(2 * i + 1, parity=1)
                step(2 * i + 2, parity=0)
            step(B - 3, parity=1)
            step(B - 2, parity=0, ahead=False)
            last_step(B - 1)

        block = ctx.enter_context(nc.Block())

        @block.sync
        def _(sp):
            def load_xT(n):
                sp.dma_start(xT_raw[:, :, :], xT_cols[n, :, :, :]).then_inc(xT_loaded, 16)

            def load_x(n):
                sp.dma_start(xb[:, :, :], x_rows[n, :, :, :]).then_inc(x_loaded, 16)

            def store(b, parity):
                sp.wait_ge(normed["out"], R * (b + 1))
                sp.dma_start(out_rows[b, :, :, :], hb[:, parity, :, :]).then_inc(out_stored, 16)

            def copy_k(n, half):
                sp.wait_ge(hi["k"], 2 * n + half + 1)
                for i in range(2):
                    heads = slice(4 * half + i, 4 * half + i + 3, 2)
                    sp.dma_start(k_twice[(1 - i) * HALF:(2 - i) * HALF, heads, :].bitcast(F32),
                                 k_twice[i * HALF:(i + 1) * HALF, heads, :].bitcast(F32)).then_inc(k_copied[half], 16)

            def step(b, parity, y_=True, ahead=True):
                if ahead:
                    sp.wait_ge(xT_split, b + 2)
                    load_xT(b + 2)
                sp.wait_ge(read["mi"], R * (b + 1))
                load_x(b + 1)
                copy_k(b + 1, 0)
                copy_k(b + 1, 1)
                if y_:
                    store(b - 1, 1 - parity)

            def load_weight(i):
                if i >= 2:
                    sp.wait_ge(w_split, i - 1)
                sp.dma_start(stage_of(i), w_dram[WEIGHTS[i]].rearrange("(c p) o -> p c o",
                                                                       p=P)).then_inc(w_loaded[WEIGHTS[i]], 16)

            load_xT(0)
            load_weight(0)
            load_weight(1)
            sp.dma_start(adjT_i.rearrange("p (r n) -> p r n", r=R),
                         adjT.rearrange("(r p) n -> p r n", p=P)).then_inc(const_loaded, 16)
            sp.dma_start(adj_i.rearrange("p (r n) -> p r n", r=R),
                         adj.rearrange("(r p) n -> p r n", p=P)).then_inc(const_loaded, 16)
            sp.dma_start(b0_rows, b0.partition_broadcast(P)).then_inc(const_loaded, 16)
            sp.wait_ge(xT_split, 1)
            load_xT(1)
            load_weight(2)
            load_weight(3)
            sp.wait_ge(adj_ready, 3)
            load_x(0)
            sp.dma_start(bo_rows[:, :], bo.partition_broadcast(P)).then_inc(bias_loaded, 16)
            sp.dma_start(bq_cols[:, :], bq).then_inc(bias_loaded, 16)
            sp.dma_start(bk_cols[:, :], bk).then_inc(bias_loaded, 16)
            sp.dma_start(bv_cols[:, :], bv).then_inc(bias_loaded, 16)
            load_weight(4)
            load_weight(5)
            copy_k(0, 0)
            copy_k(0, 1)
            steps(sp, step, lambda b: store(b - 1, 0))
            store(B - 1, (B - 1) % 2)
            sp.wait_ge(out_stored, 16 * B)

        @block.gpsimd
        def _(pool):
            def xT_high(n):
                pool.wait_ge(xT_loaded, 16 * (n + 1))
                if type(n) is not int or n > 0:
                    pool.wait_ge(done["mi"], R * n)
                pool.tensor_tensor(xT_hi[:, :, :].rearrange("p c n -> p (c n)"),
                                   xT_raw[:, :, :].rearrange("p c n -> p (c n)"),
                                   zero[:, :].to_broadcast([P, C * N]), ALU.add).then_inc(xT_hi_done, 1)

            def normalise_odd(b, g):
                pool.wait_ge(inv_done, G * b + g + 1)
                pool.tensor_tensor(probs[:, g % 2, 1, :, :], probs[:, g % 2, 1, :, :],
                                   row_inv[:, g % 2, R:2 * R].unsqueeze(2).to_broadcast([P, R, N]),
                                   ALU.mult).then_inc(norm_odd_done, 1)

            def split_xT(n):
                pool.wait_ge(xT_hi_done, n + 1)
                pool.tensor_tensor(xT_lo[:, :, :], xT_raw[:, :, :], xT_hi[:, :, :].bitcast(F32),
                                   ALU.subtract).then_inc(xT_split, 1)

            def add_bias(n):
                pool.wait_ge(x_loaded, 16 * (n + 1))
                pool.tensor_tensor(xb[:, :, :], xb[:, :, :], deg_b0[:, :, :], ALU.add).then_inc(xb_ready, 1)

            def residual(n, parity, stored):
                pool.wait_ge(normed["h"], R * (n + 1))
                if stored:
                    pool.wait_ge(out_stored, 16 * (n - 1))
                for r in range(R):
                    last = pool.tensor_tensor(hb[:, parity, r, :], h[:, r, :], bo_rows[:, :], ALU.add)
                last.then_inc(hb_ready, 1)

            def root(which, n):
                pool.wait_ge(aggr_done[which], R * n + R)
                pool.tensor_tensor(var_eps[which][:, :], mean_var[which][:, :, 1], eps_cols[:, :],
                                   ALU.add).then_inc(var_eps_done[which], 1)
                pool.wait_ge(var_eps_done[which], n + 1)
                pool.tensor_tensor(rstd[which][:, :], var_eps[which][:, :], power_cols[:, :],
                                   ALU.pow).then_inc(rstd_done[which], 1)

            def split_o(b, g):
                pool.wait_ge(o_hi_done, G * b + g + 1)
                pool.tensor_tensor(oT_lo[:, g, :], oT[:, :], oT_hi[:, g, :].bitcast(F32),
                                   ALU.subtract).then_inc(o_split, 1)

            pool.memset(ident[:, :], 0.0).then_inc(zeroed, 1)
            pool.wait_ge(zeroed, 1)
            pool.affine_select(out=ident[:, :], in_=ident[:, :], compare_op=ALU.not_equal, fill=1.0, base=0,
                               pattern=[[-1, P]], channel_multiplier=1).then_inc(ident_ready, 1)
            pool.memset(eps_cols[:, :], EPS).then_inc(zeroed, 1)
            pool.memset(power_cols[:, :], -0.5).then_inc(zeroed, 1)
            pool.memset(zero[:, :], 0.0).then_inc(zeroed, 1)
            pool.wait_ge(zeroed, 4)
            xT_high(0)
            split_xT(0)
            pool.wait_ge(deg_b0_ready, R)
            add_bias(0)
            root("h", 0)
            xT_high(1)
            split_xT(1)
            pool.wait_ge(bias_loaded, 64)
            pool.wait_ge(w_split, len(WEIGHTS))
            residual(0, 0, stored=False)

            def step(b, parity, y_=True, ahead=True):
                n = b + 1
                add_bias(n)
                normalise_odd(b, 0)
                root("h", n)
                normalise_odd(b, 1)
                normalise_odd(b, 2)
                if ahead: xT_high(b + 2)
                if ahead: split_xT(b + 2)
                split_o(b, 0)
                normalise_odd(b, 3)
                if y_: root("out", b - 1)
                split_o(b, 1)
                split_o(b, 2)
                residual(n, 1 - parity, stored=y_)
                split_o(b, 3)

            def last_step(b):
                normalise_odd(b, 0)
                normalise_odd(b, 1)
                normalise_odd(b, 2)
                split_o(b, 0)
                normalise_odd(b, 3)
                root("out", b - 1)
                split_o(b, 1)
                split_o(b, 2)
                split_o(b, 3)

            steps(pool, step, last_step)
            root("out", B - 1)

        @block.tensor
        def _(pe):
            def mm(dst, lhsT, rhs, start, stop):
                return pe.matmul(dst, lhsT, rhs, start=start, stop=stop)

            def product(dst, l_hi, l_lo, r_hi, r_lo):
                terms = [(a(c), b(c)) for c in range(C) for a, b in ((l_hi, r_hi), (l_lo, r_hi), (l_hi, r_lo))]
                for i, (a, b) in enumerate(terms):
                    last = mm(dst, a, b, i == 0, i == len(terms) - 1)
                return last

            def rows_times_w(kind, r, l_hi, l_lo, w):
                rows = slice(r * P, (r + 1) * P)
                product(proj[BANK[kind][r]][:, :], lambda c: l_hi[:, c, rows], lambda c: l_lo[:, c, rows],
                        lambda c: w_hi[w][:, c, :], lambda c: w_lo[w][:, c, :]).then_inc(done[kind], 1)

            def mj(n, r, first=False):
                if r == 0:
                    pe.wait_ge(xT_split, n + 1)
                    if first:
                        pe.wait_ge(w_split, 1)
                    else:
                        pe.wait_ge(read["k"], 2 * n - 1)
                elif not first:
                    pe.wait_ge(read["v"], R * n)
                rows_times_w("mj", r, xT_hi, xT_lo, "wj")

            def mi(n, r, first=False):
                if first and r == 0:
                    pe.wait_ge(w_split, 2)
                if r == 1:
                    pe.wait_ge(read["mj"], R * n + 1)
                rows_times_w("mi", r, xT_hi, xT_lo, "wi")

            def aggregate(n, r):
                if r == 0:
                    pe.wait_ge(read["mj"], R * n + 2)
                else:
                    pe.wait_ge(read["mi"], R * n + 1)
                terms = [(aT[:, j, r * P:(r + 1) * P], half[:, j, :]) for j in range(R) for half in (mj_hi, mj_lo)]
                for i, (a, m) in enumerate(terms):
                    last = mm(proj[BANK["agg"][r]][:, :], a, m, i == 0, i == len(terms) - 1)
                last.then_inc(done["agg"], 1)

            def y(b, r, tail=False):
                if r == 0:
                    pe.wait_ge(o_split, G * (b + 1))
                if r == 0 and not tail:
                    pe.wait_ge(read["mi"], R * (b + 3))
                elif r == 1 and not tail:
                    pe.wait_ge(read["agg"], R * (b + 2) + 1)
                elif r == 1:
                    pe.wait_ge(read["v"], R * (b + 2))
                rows_times_w("y", r, oT_hi, oT_lo, "wo")

            def last_y():
                passes = [(oT_hi, w_hi["wo"]), (oT_lo, w_hi["wo"]), (oT_hi, w_lo["wo"])]
                for c in range(C):
                    if c in (0, C - 1):
                        pe.wait_ge(o_split, G * (B - 1) + (C - 1 if c == 0 else C))
                    for r in range(R):
                        for i, (o, w) in enumerate(passes):
                            last = mm(proj[BANK["y"][r]][:, :], o[:, c, r * P:(r + 1) * P], w[:, c, :],
                                      c == 0 and i == 0, c == C - 1 and i == len(passes) - 1)
                        if c == C - 1:
                            last.then_inc(done["y"], 1)

            def transpose_h(n, half, first=False):
                if half == 0:
                    pe.wait_ge(normed["h"], R * (n + 1))
                elif type(n) is not int or n >= 2:
                    pe.wait_ge(read["y"], R * (n - 2) + 1)
                if first:
                    pe.wait_ge(ident_ready, 1)
                dst = proj[BANK["hT"][half]][:, :].rearrange("p (c n) -> p c n", c=2)
                for c in range(2):
                    for r in range(R):
                        last = pe.transpose(dst[:, c, r * P:(r + 1) * P],
                                            h[:, r, (2 * half + c) * P:(2 * half + c + 1) * P], ident[:, :])
                last.then_inc(done["hT"], 1)

            def cols_of(kind, n, half, w):
                dst = proj[BANK[kind][half]][:, :].rearrange("p (c n) -> p c n", c=2)
                for c in range(2):
                    cols = slice((2 * half + c) * P, (2 * half + c + 1) * P)
                    last = product(dst[:, c, :], lambda k: w_hi[w][:, k, cols], lambda k: w_lo[w][:, k, cols],
                                   lambda k: hT_hi[:, k, :], lambda k: hT_lo[:, k, :])
                last.then_inc(done[kind], 1)

            def q(n, half, first=False):
                if first:
                    pe.wait_ge(w_split, 3)
                if half == 0:
                    pe.wait_ge(read["hT"], 2 * n + 2)
                    if type(n) is not int or n >= 2:
                        pe.wait_ge(read["y"], R * (n - 1))
                cols_of("q", n, half, "wq")

            def k(n, half, first=False):
                if first:
                    pe.wait_ge(w_split, 4)
                if half == 1:
                    pe.wait_ge(read["q"], 2 * n + 1)
                cols_of("k", n, half, "wk")

            def v(n, r, first=False):
                if first:
                    pe.wait_ge(w_split, 5)
                if r == 0:
                    pe.wait_ge(read["q"], 2 * n + 2)
                else:
                    pe.wait_ge(read["k"], 2 * n + 2)
                rows_times_w("v", r, hT_hi, hT_lo, "wv")

            def scores(b, g, first=False):
                pe.wait_ge(read["q"], 2 * b + g // 2 + 1)
                pe.wait_ge(read["k"], 2 * b + g // 2 + 1)
                pe.wait_ge(k_copied[g // 2], 32 * (b + 1))
                if not (first and g == 0):
                    pe.wait_ge(max_done, 2 * (G * b + g))
                blocks = [(i, r) for i in range(2) for r in range(R)]
                for i, r in blocks:
                    head = 2 * g + i
                    pe.matmul(score[i][:, r * N:(r + 1) * N], q_both[:, head, r * P:(r + 1) * P],
                              k_twice[:, head, :], start=(r == 0), stop=False, skip_group_check=True)
                for i, r in [(i, r) for r in range(R) for i in range(2)]:
                    head, home = 2 * g + i, slice(i * HALF, (i + 1) * HALF)
                    last = pe.matmul(score[i][:, r * N:(r + 1) * N], q_both[home, head, r * P:(r + 1) * P],
                                     k_lo[home, g, :], start=False, stop=True, skip_group_check=True)
                    if r == R - 1:
                        last.then_inc(score_done, 1)

            def transpose_p(b, g, i, first=False):
                pe.wait_ge((norm_even_done, norm_odd_done)[i], G * b + g + 1)
                if not (first and g == 0):
                    pe.wait_ge(pt_read, 2 * (G * b + g) + i - 1)
                dst = pt[i][:, :].rearrange("p (k q) -> p k q", k=R)
                for kt in range(R):
                    for r in range(R):
                        last = pe.transpose(dst[:, kt, r * P:(r + 1) * P],
                                            probs[:, g % 2, i, r, kt * P:(kt + 1) * P], ident[:, :])
                last.then_inc(pt_done, 1)

            def attend(b, g, first=False):
                if g == 0:
                    pe.wait_ge(read["v"], R * (b + 1))
                pe.wait_ge(pt_read, 2 * (G * b + g) + 2)
                if not (first and g == 0):
                    pe.wait_ge(av_read, G * b + g)
                for i in range(2):
                    terms = [(kt, half) for kt in range(R) for half in (pT_hi, pT_lo)]
                    for j, (kt, half) in enumerate(terms):
                        last = mm(av[:, i * N:(i + 1) * N], v_both[:, kt, 2 * g + i, :], half[:, i, kt, :],
                                  j == 0, j == len(terms) - 1)
                last.then_inc(av_done, 1)

            def step(b, parity, y_=True, ahead=True):
                n = b + 1
                mj(n, 0)
                scores(b, 0, not y_)
                mj(n, 1)
                mi(n, 0)
                scores(b, 1)
                mi(n, 1)
                aggregate(n, 0)
                aggregate(n, 1)
                transpose_p(b, 0, 0, not y_)
                transpose_p(b, 0, 1, not y_)
                scores(b, 2)
                if y_: y(b - 1, 0)
                if y_: y(b - 1, 1)
                transpose_h(n, 0)
                transpose_h(n, 1)
                scores(b, 3)
                transpose_p(b, 1, 0)
                transpose_p(b, 1, 1)
                attend(b, 0, not y_)
                q(n, 0)
                q(n, 1)
                transpose_p(b, 2, 0)
                transpose_p(b, 2, 1)
                attend(b, 1)
                k(n, 0)
                k(n, 1)
                transpose_p(b, 3, 0)
                attend(b, 2)
                transpose_p(b, 3, 1)
                v(n, 0)
                v(n, 1)
                attend(b, 3)

            for r in range(R):
                mj(0, r, first=True)
            for r in range(R):
                mi(0, r, first=True)
            pe.wait_ge(adj_ready, 1)
            for r in range(R):
                aggregate(0, r)
            for half in range(2):
                transpose_h(0, half, first=True)
            for half in range(2):
                q(0, half, first=True)
            for half in range(2):
                k(0, half, first=True)
            for r in range(R):
                v(0, r, first=True)
            pe.wait_ge(w_split, len(WEIGHTS))
            def last_step(b):
                scores(b, 0)
                scores(b, 1)
                transpose_p(b, 0, 0)
                transpose_p(b, 0, 1)
                scores(b, 2)
                y(b - 1, 0, tail=True)
                scores(b, 3)
                transpose_p(b, 1, 0)
                transpose_p(b, 1, 1)
                attend(b, 0)
                y(b - 1, 1, tail=True)
                transpose_p(b, 2, 0)
                attend(b, 1)
                transpose_p(b, 2, 1)
                attend(b, 2)
                transpose_p(b, 3, 0)
                transpose_p(b, 3, 1)
                attend(b, 3)

            steps(pe, step, last_step)
            last_y()

        @block.scalar
        def _(act):
            def copy_hi(kind, n, tile, dst, src):
                act.wait_ge(done[kind], 2 * n + tile + 1)
                nc.scalar.copy(dst, src).then_inc(hi[kind], 1)

            def mj_high(n, r):
                copy_hi("mj", n, r, mj_hi[:, r, :], proj[BANK["mj"][r]][:, :])

            def hT_high(n, half):
                copy_hi("hT", n, half, hT_hi[:, 2 * half:2 * half + 2, :],
                        proj[BANK["hT"][half]][:, :].rearrange("p (c n) -> p c n", c=2))

            def v_high(n, r):
                if r == 0 and not (type(n) is int and n == 0):
                    act.wait_ge(av_done, G * n)
                copy_hi("v", n, r, v_both[:, r, :, 0:DH],
                        proj[BANK["v"][r]][:, :].rearrange("p (h d) -> p h d", h=HEADS))

            def heads_used(n, half):
                if not (type(n) is int and n == 0):
                    act.wait_ge(score_done, 2 * G * (n - 1) + G * (half + 1))

            def q_high(n, half):
                heads_used(n, half)
                act.wait_ge(done["q"], 2 * n + half + 1)
                for c in range(2):
                    t = 2 * half + c
                    src = proj[BANK["q"][half]][:, c * N:(c + 1) * N]
                    for i in range(2):
                        home = slice(i * HALF, (i + 1) * HALF)
                        last = nc.scalar.activation(q_both[home, 2 * t + i, :], src[home, :], ACT.Identity,
                                                    bias=bq_cols[home, t:t + 1])
                last.then_inc(hi["q"], 1)

            def k_high(n, half):
                heads_used(n, half)
                act.wait_ge(done["k"], 2 * n + half + 1)
                for c in range(2):
                    t = 2 * half + c
                    src = proj[BANK["k"][half]][:, c * N:(c + 1) * N]
                    for i in range(2):
                        home = slice(i * HALF, (i + 1) * HALF)
                        last = nc.scalar.activation(k_twice[home, 2 * t + i, :], src[home, :], ACT.Identity,
                                                    bias=bk_cols[home, t:t + 1])
                last.then_inc(hi["k"], 1)

            def exponentials(b, g):
                act.wait_ge(bias_done, G * b + g + 1)
                for i in range(2):
                    for r in range(R):
                        s = R * i + r
                        e = probs[:, g % 2, i, r, :]
                        last = nc.scalar.activation(e, e, ACT.Exp, bias=exp_bias[:, g % 2, s:s + 1], scale=SCALE,
                                                    accum_out=row_sum[:, g % 2, s:s + 1])
                last.then_inc(exp_done, 1)

            def normalise_even(b, g):
                act.wait_ge(inv_done, G * b + g + 1)
                for r in range(R):
                    e = probs[:, g % 2, 0, r, :]
                    last = nc.scalar.activation(e, e, ACT.Copy, scale=row_inv[:, g % 2, r:r + 1])
                last.then_inc(norm_even_done, 1)

            def pt_high(b, g, i, first=False):
                act.wait_ge(pt_done, 2 * (G * b + g) + i + 1)
                if i == 0 and not (first and g == 0):
                    act.wait_ge(av_done, G * b + g)
                nc.scalar.copy(pT_hi[:, i, :, :],
                               pt[i][:, :].rearrange("p (k q) -> p k q", k=R)).then_inc(pt_hi_done, 1)

            def o_low_part(b, g, first=False):
                act.wait_ge(av_done, G * b + g + 1)
                if not (first and g == 0):
                    act.wait_ge(av_read, G * b + g)
                nc.scalar.copy(o_part[:, :, :],
                               av[HALF:P, :].rearrange("p (i n) -> p i n", i=2)).then_inc(o_part_done, 1)

            def o_high(b, g, first=False):
                act.wait_ge(av_read, G * b + g + 1)
                if g == 0 and not first:
                    act.wait_ge(done["y"], R * b)
                nc.scalar.copy(oT_hi[:, g, :], oT[:, :]).then_inc(o_hi_done, 1)

            def step(b, parity, y_=True, ahead=True):
                n = b + 1
                mj_high(n, 0)
                exponentials(b, 0)
                mj_high(n, 1)
                normalise_even(b, 0)
                exponentials(b, 1)
                pt_high(b, 0, 0, not y_)
                normalise_even(b, 1)
                pt_high(b, 0, 1, not y_)
                exponentials(b, 2)
                hT_high(n, 0)
                hT_high(n, 1)
                normalise_even(b, 2)
                pt_high(b, 1, 0)
                pt_high(b, 1, 1)
                o_low_part(b, 0, not y_)
                exponentials(b, 3)
                q_high(n, 0)
                q_high(n, 1)
                o_high(b, 0, not y_)
                o_low_part(b, 1)
                pt_high(b, 2, 0)
                pt_high(b, 2, 1)
                normalise_even(b, 3)
                k_high(n, 0)
                k_high(n, 1)
                o_high(b, 1)
                pt_high(b, 3, 0)
                pt_high(b, 3, 1)
                o_low_part(b, 2)
                v_high(n, 0)
                v_high(n, 1)
                o_high(b, 2)
                o_low_part(b, 3)
                o_high(b, 3)

            def split_weight(i):
                act.wait_ge(w_loaded[WEIGHTS[i]], 16)
                nc.scalar.copy(w_hi[WEIGHTS[i]][:, :, :], stage_of(i)).then_inc(w_hi_done, 1)

            split_weight(0)
            split_weight(1)
            mj_high(0, 0)
            mj_high(0, 1)
            for i in range(2, 5):
                split_weight(i)
            hT_high(0, 0)
            hT_high(0, 1)
            act.wait_ge(bias_loaded, 64)
            q_high(0, 0)
            q_high(0, 1)
            split_weight(5)
            k_high(0, 0)
            k_high(0, 1)
            v_high(0, 0)
            v_high(0, 1)
            def last_step(b):
                exponentials(b, 0)
                normalise_even(b, 0)
                exponentials(b, 1)
                pt_high(b, 0, 0)
                pt_high(b, 0, 1)
                normalise_even(b, 1)
                exponentials(b, 2)
                normalise_even(b, 2)
                pt_high(b, 1, 0)
                pt_high(b, 1, 1)
                o_low_part(b, 0)
                exponentials(b, 3)
                o_high(b, 0)
                o_low_part(b, 1)
                pt_high(b, 2, 0)
                pt_high(b, 2, 1)
                o_high(b, 1)
                normalise_even(b, 3)
                o_low_part(b, 2)
                pt_high(b, 3, 0)
                pt_high(b, 3, 1)
                o_high(b, 2)
                o_low_part(b, 3)
                o_high(b, 3)

            steps(act, step, last_step)

        @block.vector
        def _(dve):
            V = nc.vector

            def low(kind, n, tile, dst, src, high):
                dve.wait_ge(hi[kind], 2 * n + tile + 1)
                V.tensor_tensor(dst, src, high.bitcast(F32), ALU.subtract).then_inc(read[kind], 1)

            def mj_low(n, r):
                low("mj", n, r, mj_lo[:, r, :], proj[BANK["mj"][r]][:, :], mj_hi[:, r, :])

            def hT_low(n, half):
                cs = slice(2 * half, 2 * half + 2)
                low("hT", n, half, hT_lo[:, cs, :],
                    proj[BANK["hT"][half]][:, :].rearrange("p (c n) -> p c n", c=2), hT_hi[:, cs, :])

            def v_low(n, r):
                low("v", n, r, v_both[:, r, :, DH:2 * DH],
                    proj[BANK["v"][r]][:, :].rearrange("p (h d) -> p h d", h=HEADS), v_both[:, r, :, 0:DH])

            def biased_low(kind, n, half, bias, high, dst):
                dve.wait_ge(hi[kind], 2 * n + half + 1)
                for c in range(2):
                    t = 2 * half + c
                    src = proj[BANK[kind][half]][:, c * N:(c + 1) * N]
                    for i in range(2):
                        home = slice(i * HALF, (i + 1) * HALF)
                        last = V.scalar_tensor_tensor(
                            out=dst(t, i), in0=src[home, :], scalar=bias[home, t:t + 1],
                            in1=high[home, 2 * t + i, :].bitcast(F32), op0=ALU.add, op1=ALU.subtract)
                last.then_inc(read[kind], 1)

            def q_low(n, half):
                biased_low("q", n, half, bq_cols, q_both,
                           lambda t, i: q_both[(1 - i) * HALF:(2 - i) * HALF, 2 * t + i, :])

            def k_low_half(n, half):
                biased_low("k", n, half, bk_cols, k_twice,
                           lambda t, i: k_lo[i * HALF:(i + 1) * HALF, t, :])

            def maxima(b, g, first=False):
                for i in range(2):
                    dve.wait_ge(score_done, 2 * (G * b + g) + i + 1)
                    if i == 0 and not (first and g < 2):
                        dve.wait_ge(pt_done, 2 * (G * b + g) - 2)
                    dve.nop(nofuse=True)
                    for r in range(R):
                        s = R * i + r
                        last = V.tensor_tensor_reduce(
                            out=probs[:, g % 2, i, r, :], in0=score[i][:, r * N:(r + 1) * N],
                            in1=mask_add[:, r, :], scale=1.0, scalar=MASKED, op0=ALU.add, op1=ALU.max,
                            accum_out=row_max[:, g % 2, s:s + 1])
                    last.then_inc(max_done, 1)
                dve.wait_ge(max_done, 2 * (G * b + g) + 2)
                V.tensor_scalar(exp_bias[:, g % 2, :], row_max[:, g % 2, :], MAX_FLOOR, -SCALE,
                                ALU.max, ALU.mult).then_inc(bias_done, 1)

            def inverse_sums(b, g):
                dve.wait_ge(exp_done, G * b + g + 1)
                V.reciprocal(row_inv[:, g % 2, :], row_sum[:, g % 2, :]).then_inc(inv_done, 1)

            def pt_low(b, g, i):
                dve.wait_ge(pt_hi_done, 2 * (G * b + g) + i + 1)
                V.tensor_tensor(pT_lo[:, i, :, :], pt[i][:, :].rearrange("p (k q) -> p k q", k=R),
                                pT_hi[:, i, :, :].bitcast(F32), ALU.subtract).then_inc(pt_read, 1)

            def o_sum(b, g, first=False):
                dve.wait_ge(o_part_done, G * b + g + 1)
                if not (first and g == 0):
                    dve.wait_ge(o_split, G * b + g)
                for i in range(2):
                    last = V.scalar_tensor_tensor(
                        out=oT[i * HALF:(i + 1) * HALF, :], in0=av[0:HALF, i * N:(i + 1) * N],
                        scalar=bv_cols[:, 2 * g + i:2 * g + i + 1], in1=o_part[:, i, :],
                        op0=ALU.add, op1=ALU.add)
                last.then_inc(av_read, 1)

            def mi_sum(n, r, first=False):
                dve.wait_ge(done["mi"], R * n + r + 1)
                dve.wait_ge(xb_ready, n + 1)
                if not first:
                    dve.wait_ge(hb_ready, n)
                V.scalar_tensor_tensor(out=h[:, r, :], in0=proj[BANK["mi"][r]][:, :], scalar=deg[:, r:r + 1],
                                       in1=xb[:, r, :], op0=ALU.mult, op1=ALU.add).then_inc(read["mi"], 1)

            def agg_sum(n, r):
                dve.wait_ge(done["agg"], R * n + r + 1)
                dve.wait_ge(read["mi"], R * n + r + 1)
                V.tensor_tensor(h[:, r, :], proj[BANK["agg"][r]][:, :], h[:, r, :],
                                ALU.add).then_inc(read["agg"], 1)

            def y_sum(b, r, parity):
                dve.wait_ge(done["y"], R * b + r + 1)
                dve.wait_ge(hb_ready, b + 1)
                V.tensor_tensor(hb[:, parity, r, :], proj[BANK["y"][r]][:, :], hb[:, parity, r, :],
                                ALU.add).then_inc(read["y"], 1)

            h_row = lambda r: h[:, r, :]
            hb_row = [lambda r: hb[:, 0, r, :], lambda r: hb[:, 1, r, :]]

            def norm_stats(which, n, r, summed, row):
                dve.wait_ge(summed, R * n + r + 1)
                V.bn_stats(stats[which][:, r, :], row(r)).then_inc(stats_done[which], 1)

            def norm_mean(which, n):
                dve.wait_ge(stats_done[which], R * n + R)
                dve.nop(nofuse=True)
                for r in range(R):
                    V.bn_aggr(mean_var[which][:, r, :], stats[which][:, r, :]).then_inc(aggr_done[which], 1)

            def norm_apply(which, n, row):
                dve.wait_ge(rstd_done[which], n + 1)
                for r in range(R):
                    V.tensor_scalar(row(r), row(r), mean_var[which][:, r, 0:1], rstd[which][:, r:r + 1],
                                    ALU.subtract, ALU.mult).then_inc(normed[which], 1)

            def step(b, parity, y_=True, ahead=True):
                n, other = b + 1, 1 - parity
                maxima(b, 0, not y_)
                mj_low(n, 0)
                mi_sum(n, 0)
                mj_low(n, 1)
                inverse_sums(b, 0)
                maxima(b, 1, not y_)
                mi_sum(n, 1)
                agg_sum(n, 0)
                agg_sum(n, 1)
                norm_stats("h", n, 0, read["agg"], h_row)
                norm_stats("h", n, 1, read["agg"], h_row)
                inverse_sums(b, 1)
                norm_mean("h", n)
                maxima(b, 2)
                norm_apply("h", n, h_row)
                if y_: y_sum(b - 1, 0, other)
                pt_low(b, 0, 0)
                pt_low(b, 0, 1)
                if y_: y_sum(b - 1, 1, other)
                inverse_sums(b, 2)
                hT_low(n, 0)
                hT_low(n, 1)
                maxima(b, 3)
                if y_: norm_stats("out", b - 1, 0, read["y"], hb_row[other])
                pt_low(b, 1, 0)
                pt_low(b, 1, 1)
                o_sum(b, 0, not y_)
                inverse_sums(b, 3)
                if y_: norm_stats("out", b - 1, 1, read["y"], hb_row[other])
                q_low(n, 0)
                q_low(n, 1)
                o_sum(b, 1)
                pt_low(b, 2, 0)
                pt_low(b, 2, 1)
                if y_: norm_mean("out", b - 1)
                k_low_half(n, 0)
                k_low_half(n, 1)
                pt_low(b, 3, 0)
                o_sum(b, 2)
                pt_low(b, 3, 1)
                if y_: norm_apply("out", b - 1, hb_row[other])
                v_low(n, 0)
                v_low(n, 1)
                o_sum(b, 3)

            def split_weight(i):
                dve.wait_ge(w_hi_done, i + 1)
                V.tensor_tensor(w_lo[WEIGHTS[i]][:, :, :], stage_of(i), w_hi[WEIGHTS[i]][:, :, :].bitcast(F32),
                                ALU.subtract).then_inc(w_split, 1)

            split_weight(0)
            split_weight(1)

            dve.wait_ge(const_loaded, 48)
            V.tensor_copy(aT[:, :, :], adjT_i.rearrange("p (r n) -> p r n", r=R)).then_inc(adj_ready, 1)
            V.tensor_copy(adj_f, adj_i).then_inc(adj_ready, 1)
            dve.wait_ge(adj_ready, 2)
            V.tensor_scalar(mask_add[:, :, :], adj_f.rearrange("p (r n) -> p r n", r=R), 0.0, MASKED,
                            ALU.is_equal, ALU.mult).then_inc(adj_ready, 1)
            V.tensor_reduce(deg[:, :], adj_f.rearrange("p (r n) -> p r n", r=R), AX_X, ALU.add).then_inc(deg_ready, 1)
            dve.wait_ge(deg_ready, 1)
            for r in range(R):
                V.tensor_scalar(deg_b0[:, r, :], b0_rows, deg[:, r:r + 1], None, ALU.mult).then_inc(deg_b0_ready, 1)
            mj_low(0, 0)
            mj_low(0, 1)
            split_weight(2)
            dve.wait_ge(deg_b0_ready, R)
            mi_sum(0, 0, first=True)
            mi_sum(0, 1, first=True)
            for r in range(R):
                agg_sum(0, r)
                norm_stats("h", 0, r, read["agg"], h_row)
            norm_mean("h", 0)
            split_weight(3)
            norm_apply("h", 0, h_row)
            hT_low(0, 0)
            hT_low(0, 1)
            split_weight(4)
            dve.wait_ge(bias_loaded, 64)
            q_low(0, 0)
            q_low(0, 1)
            split_weight(5)
            k_low_half(0, 0)
            k_low_half(0, 1)
            v_low(0, 0)
            v_low(0, 1)
            def last_step(b):
                maxima(b, 0)
                inverse_sums(b, 0)
                maxima(b, 1)
                inverse_sums(b, 1)
                maxima(b, 2)
                pt_low(b, 0, 0)
                pt_low(b, 0, 1)
                y_sum(b - 1, 0, 0)
                inverse_sums(b, 2)
                maxima(b, 3)
                pt_low(b, 1, 0)
                pt_low(b, 1, 1)
                o_sum(b, 0)
                norm_stats("out", b - 1, 0, read["y"], hb_row[0])
                y_sum(b - 1, 1, 0)
                inverse_sums(b, 3)
                norm_stats("out", b - 1, 1, read["y"], hb_row[0])
                norm_mean("out", b - 1)
                o_sum(b, 1)
                pt_low(b, 2, 0)
                pt_low(b, 2, 1)
                norm_apply("out", b - 1, hb_row[0])
                o_sum(b, 2)
                pt_low(b, 3, 0)
                pt_low(b, 3, 1)
                o_sum(b, 3)

            steps(dve, step, last_step)
            for r in range(R):
                y_sum(B - 1, r, 1)
                norm_stats("out", B - 1, r, read["y"], hb_row[1])
            norm_mean("out", B - 1)
            norm_apply("out", B - 1, hb_row[1])


def kernel(**inputs):
    import numpy as np
    import concourse.bacc as bacc
    from concourse.bass_utils import run_bass_kernel_spmd

    def array(name):
        return np.asarray(inputs[name])

    def columns(a, p):
        return a.reshape(-1, p).T

    x, adj, w0 = array("x"), array("adj"), array("L0_gnn_W")
    laid_out = {
        "x": x, "xT": x.transpose(0, 2, 1), "adj": adj, "adjT": adj.T,
        "w0T": w0.T, "b0": array("L0_gnn_b"),
        "wqT": array("L1_gnn_Wq").T, "wkT": array("L1_gnn_Wk").T,
        "wvT": array("L1_gnn_Wv").T, "woT": array("L1_gnn_Wo").T,
        "bq": columns(array("L1_gnn_bq"), P), "bk": columns(array("L1_gnn_bk"), P),
        "bv": columns(array("L1_gnn_bv"), P // 2), "bo": array("L1_gnn_bo"),
    }
    nc = bacc.Bacc("TRN2", target_bir_lowering=False, num_devices=1)
    arrays, args = {}, []
    for name, a in laid_out.items():
        a = np.ascontiguousarray(a)
        arrays[f"in_{name}"] = a
        args.append(nc.dram_tensor(f"in_{name}", a.shape, mybir.dt.from_np(a.dtype), kind="ExternalInput").ap())
    args.append(nc.dram_tensor("out_0", x.shape, F32, kind="ExternalOutput").ap())
    build(nc, *args)
    r = run_bass_kernel_spmd(nc, [arrays], core_ids=[0])
    return r.results[0]["out_0"]
```
